# Optimizing a Trainium2 kernel written in Bass

```python
import numpy as np
import jax
import jax.numpy as jnp

def _softmax(x, axis=-1):
    return jax.nn.softmax(x, axis=axis)

def _gelu(x):
    return jax.nn.gelu(x, approximate=True)

def _silu(x):
    return jax.nn.silu(x)

def _sigmoid(x):
    return jax.nn.sigmoid(x)

def _layernorm(x, axis=-1, eps=1e-05):
    m = jnp.mean(x, axis=axis, keepdims=True)
    v = jnp.var(x, axis=axis, keepdims=True)
    return (x - m) / jnp.sqrt(v + eps)

def _scatter_add(tgt, idx, src, axis=0):
    return tgt.at[idx].add(src)

def _segment_sum(src, seg, n):
    return jax.ops.segment_sum(src, seg, n)
kernel_name = 'mk_macaron_d1_jaxref_r8_f08bbd'

def setup_inputs(seed: int=0):
    np.random.seed(seed)
    _w = jnp.asarray

    def _L0_attn_setup():
        import jax, jax.numpy as jnp
        import numpy as np
        HEADS, KV_HEADS, HEAD_DIM = (16, 4, 128)
        WINDOW, ROPE_THETA, EPS = (64, 10000.0, 1e-06)

        def _rms_norm(x, w):
            xf = x.astype(jnp.float32)
            y = xf * jax.lax.rsqrt(jnp.mean(xf * xf, axis=-1, keepdims=True) + EPS)
            return (y * (1.0 + w.astype(jnp.float32))).astype(x.dtype)

        def _rope_cos_sin(T, dtype):
            inv_freq = 1.0 / ROPE_THETA ** (jnp.arange(0, HEAD_DIM, 2, dtype=jnp.float32) / HEAD_DIM)
            pos = jnp.arange(T, dtype=jnp.float32)
            freqs = pos[:, None] * inv_freq[None, :]
            emb = jnp.concatenate([freqs, freqs], axis=-1)
            return (emb.astype(dtype), emb)

        def _rotate_half(x):
            x1, x2 = jnp.split(x, 2, axis=-1)
            return jnp.concatenate([-x2, x1], axis=-1)
        key = jax.random.key(seed)
        ks = jax.random.split(key, 7)
        B, T, D = (2, 256, 256)
        s = lambda k, shape, fan: jax.random.normal(k, shape, jnp.float32) * fan ** (-0.5)
        return {'x': jax.random.normal(ks[0], (B, T, D), jnp.float32), 'Wq': s(ks[1], (HEADS * HEAD_DIM, D), D), 'Wk': s(ks[2], (KV_HEADS * HEAD_DIM, D), D), 'Wv': s(ks[3], (KV_HEADS * HEAD_DIM, D), D), 'Wo': s(ks[4], (D, HEADS * HEAD_DIM), HEADS * HEAD_DIM), 'qn_w': jax.random.normal(ks[5], (HEAD_DIM,), jnp.float32) * 0.02, 'kn_w': jax.random.normal(ks[6], (HEAD_DIM,), jnp.float32) * 0.02}
    _L0_attn_in = _L0_attn_setup()

    def _L0_ffn_setup():
        import jax, jax.numpy as jnp
        import numpy as np
        B, S, H, I = (1, 64, 256, 768)

        def _quantized_matmul(x, w, scale):
            wq = w.astype(jnp.float8_e4m3fn).astype(x.dtype)
            y = jnp.einsum('bsi,io->bso', x, wq)
            return y * scale
        key = jax.random.key(seed)
        ks = jax.random.split(key, 7)
        return {'x': jax.random.normal(ks[0], (B, S, H), dtype=jnp.float32), 'gate_w': jax.random.normal(ks[1], (H, I), dtype=jnp.float32) * 0.02, 'up_w': jax.random.normal(ks[2], (H, I), dtype=jnp.float32) * 0.02, 'down_w': jax.random.normal(ks[3], (I, H), dtype=jnp.float32) * 0.02, 'gate_scale': jax.random.uniform(ks[4], (I,), dtype=jnp.float32, minval=0.5, maxval=1.5), 'up_scale': jax.random.uniform(ks[5], (I,), dtype=jnp.float32, minval=0.5, maxval=1.5), 'down_scale': jax.random.uniform(ks[6], (H,), dtype=jnp.float32, minval=0.5, maxval=1.5)}
    _L0_ffn_in = _L0_ffn_setup()
    _d = {'L0_attn_x': _L0_attn_in['x'], 'L0_attn_Wq': _L0_attn_in['Wq'], 'L0_attn_Wk': _L0_attn_in['Wk'], 'L0_attn_Wv': _L0_attn_in['Wv'], 'L0_attn_Wo': _L0_attn_in['Wo'], 'L0_attn_qn_w': _L0_attn_in['qn_w'], 'L0_attn_kn_w': _L0_attn_in['kn_w'], 'L0_ffn_gate_w': _L0_ffn_in['gate_w'], 'L0_ffn_up_w': _L0_ffn_in['up_w'], 'L0_ffn_down_w': _L0_ffn_in['down_w'], 'L0_ffn_gate_scale': _L0_ffn_in['gate_scale'], 'L0_ffn_up_scale': _L0_ffn_in['up_scale'], 'L0_ffn_down_scale': _L0_ffn_in['down_scale']}
    _x0 = _d['L0_attn_x']
    _d['L0_attn_x'] = jax.random.normal(jax.random.fold_in(jax.random.key(seed), 1), (16, 256, 256), dtype=_x0.dtype)
    del _x0
    return _d

def reference(L0_attn_x, L0_attn_Wq, L0_attn_Wk, L0_attn_Wv, L0_attn_Wo, L0_attn_qn_w, L0_attn_kn_w, L0_ffn_gate_w, L0_ffn_up_w, L0_ffn_down_w, L0_ffn_gate_scale, L0_ffn_up_scale, L0_ffn_down_scale):

    def _L0_attn_ref(x, Wq, Wk, Wv, Wo, qn_w, kn_w):
        import jax, jax.numpy as jnp
        import numpy as np
        HEADS, KV_HEADS, HEAD_DIM = (16, 4, 128)
        WINDOW, ROPE_THETA, EPS = (64, 10000.0, 1e-06)

        def _rms_norm(x, w):
            xf = x.astype(jnp.float32)
            y = xf * jax.lax.rsqrt(jnp.mean(xf * xf, axis=-1, keepdims=True) + EPS)
            return (y * (1.0 + w.astype(jnp.float32))).astype(x.dtype)

        def _rope_cos_sin(T, dtype):
            inv_freq = 1.0 / ROPE_THETA ** (jnp.arange(0, HEAD_DIM, 2, dtype=jnp.float32) / HEAD_DIM)
            pos = jnp.arange(T, dtype=jnp.float32)
            freqs = pos[:, None] * inv_freq[None, :]
            emb = jnp.concatenate([freqs, freqs], axis=-1)
            return (emb.astype(dtype), emb)

        def _rotate_half(x):
            x1, x2 = jnp.split(x, 2, axis=-1)
            return jnp.concatenate([-x2, x1], axis=-1)
        B, T, D = x.shape
        H, Hkv, Dh = (HEADS, KV_HEADS, HEAD_DIM)
        G = H // Hkv
        q = (x @ Wq.T).reshape(B, T, H, Dh).transpose(0, 2, 1, 3)
        k = (x @ Wk.T).reshape(B, T, Hkv, Dh).transpose(0, 2, 1, 3)
        v = (x @ Wv.T).reshape(B, T, Hkv, Dh).transpose(0, 2, 1, 3)
        q = _rms_norm(q, qn_w)
        k = _rms_norm(k, kn_w)
        emb_c, emb_f = _rope_cos_sin(T, x.dtype)
        cos = jnp.cos(emb_f).astype(x.dtype)[None, None]
        sin = jnp.sin(emb_f).astype(x.dtype)[None, None]
        q = q * cos + _rotate_half(q) * sin
        k = k * cos + _rotate_half(k) * sin
        q = q * Dh ** (-0.5)
        qg = q.reshape(B, Hkv, G, T, Dh)
        scores = jnp.einsum('bhgtd,bhkd->bhgtk', qg.astype(jnp.float32), k.astype(jnp.float32))
        dist = jnp.arange(T)[:, None] - jnp.arange(T)[None, :]
        mask = (dist >= 0) & (dist <= WINDOW)
        scores = jnp.where(mask[None, None, None], scores, jnp.finfo(jnp.float32).min)
        att = jax.nn.softmax(scores, axis=-1).astype(x.dtype)
        ctx = jnp.einsum('bhgtk,bhkd->bhgtd', att, v)
        out = ctx.reshape(B, H, T, Dh).transpose(0, 2, 1, 3).reshape(B, T, H * Dh)
        return out @ Wo.T

    def _L0_ffn_ref(x, gate_w, up_w, down_w, gate_scale, up_scale, down_scale):
        import jax, jax.numpy as jnp
        import numpy as np
        B, S, H, I = (1, 64, 256, 768)

        def _quantized_matmul(x, w, scale):
            wq = w.astype(jnp.float8_e4m3fn).astype(x.dtype)
            y = jnp.einsum('bsi,io->bso', x, wq)
            return y * scale
        gate = jax.nn.silu(_quantized_matmul(x, gate_w, gate_scale))
        up = _quantized_matmul(x, up_w, up_scale)
        fuse = gate * up
        return _quantized_matmul(fuse, down_w, down_scale)
    x = L0_attn_x
    x = x + 0.5 * _L0_ffn_ref(_layernorm(x, axis=-1), L0_ffn_gate_w, L0_ffn_up_w, L0_ffn_down_w, L0_ffn_gate_scale, L0_ffn_up_scale, L0_ffn_down_scale)
    x = x + _L0_attn_ref(_layernorm(x, axis=-1), L0_attn_Wq, L0_attn_Wk, L0_attn_Wv, L0_attn_Wo, L0_attn_qn_w, L0_attn_kn_w)
    x = x + 0.5 * _L0_ffn_ref(_layernorm(x, axis=-1), L0_ffn_gate_w, L0_ffn_up_w, L0_ffn_down_w, L0_ffn_gate_scale, L0_ffn_up_scale, L0_ffn_down_scale)
    return x

_drawn_inputs = setup_inputs


def setup_inputs(seed=0):
    import zlib

    import numpy as np

    out = dict(_drawn_inputs(seed))
    spreads = {}
    factors = {'L0_attn_qn_w': 36.671,
     'L0_attn_kn_w': 40.346,
     'L0_ffn_gate_scale': 5.414,
     'L0_ffn_up_scale': 6.299,
     'L0_ffn_down_scale': 6.111}
    for name, (base, spread) in spreads.items():
        noise = np.random.default_rng([zlib.crc32(name.encode()), seed]).standard_normal(out[name].shape)
        drawn = base * np.exp(spread * noise) if base else spread * noise
        out[name] = jnp.asarray(drawn.astype(out[name].dtype))
    for name, factor in factors.items():
        out[name] = (out[name] * factor).astype(out[name].dtype)
    return out
```

```python
from contextlib import ExitStack

import numpy as np

import concourse.bass as bass
from concourse import mybir

ALU = mybir.AluOpType
ACT = mybir.ActivationFunctionType
F32 = mybir.dt.float32
F32R = mybir.dt.float32r
BF16 = mybir.dt.bfloat16
I32 = mybir.dt.int32

P = 128
BATCH, T, D = 16, 256, 256
HEADS, KV, DH = 16, 4, 128
GROUP = HEADS // KV
WINDOW = 64
I = 768
KC = D // P
M = I // P
SUB = BATCH * T // P
QKV = (HEADS + 2 * KV) * DH
LN_EPS = 1e-5
RMS_EPS = 1e-6
MASKED = -1e30

F8_MIN_NORMAL = 2.0 ** -6
F8_MAGIC = 1.5 * 2.0 ** 20
F8_OVER = float(np.float32(2.0 ** 119 * 512 / 464))


class Phase:

    def __init__(self, nc, stack, semaphores, prefix):
        self.nc, self.stack, self.semaphores, self.prefix = nc, stack, semaphores, prefix

    def sb(self, name, shape, dt):
        return self.stack.enter_context(self.nc.sbuf_tensor(self.prefix + name, shape, dt))

    def ps(self, name, shape=(P, 512), dt=F32):
        return self.stack.enter_context(self.nc.psum_tensor(self.prefix + name, list(shape), dt))

    def sem(self, name):
        return self.semaphores.enter_context(self.nc.semaphore(self.prefix + name))


def stand(eng):
    eng.nop(nofuse=True)


def product(pe, out, parts, start=True, stop=True):
    for n, (w, x) in enumerate(parts):
        last = pe.matmul(out, w, x, start=start and n == 0, stop=stop and n == len(parts) - 1,
                         skip_group_check=True)
    return last


def three(w_hi, w_lo, x_hi, x_lo):
    return [(w_hi, x_hi), (w_hi, x_lo), (w_lo, x_hi)]


def weights_phase(nc, semaphores, dram, keep):
    with ExitStack() as stack:
        ph = Phase(nc, stack, semaphores, "w_")
        CH = 512
        RING = 4
        raw8 = ph.sb("raw8", [P, M, 3 * D], F32)
        magic = ph.sb("magic", [P, 2, 3 * D], F32)
        q8 = ph.sb("q8", [P, 2, 3 * D], F32)
        over = ph.sb("over", [P, 2, 3 * D], F32)
        raw = ph.sb("raw", [P, RING, CH], F32)
        raw_scale = ph.sb("raw_scale", [P, 2, M], F32)
        wrow = ph.sb("wrow", [P, 2, DH], F32)
        rope_raw = ph.sb("rope_raw", [P, 2, 2, DH], F32)

        ffn_loaded = ph.sem("ffn_loaded")
        x_loaded = ph.sem("x_loaded")
        rows_loaded = ph.sem("rows_loaded")
        raw_loaded = [ph.sem(f"raw_loaded{k}") for k in range(RING)]
        hi_done = ph.sem("hi_done")
        lo_done = ph.sem("lo_done")
        exponent = ph.sem("exponent")
        magic_ready = ph.sem("magic_ready")
        added = ph.sem("added")
        rounded = ph.sem("rounded")
        over_ready = ph.sem("over_ready")
        f8_ready = ph.sem("f8_ready")
        small = ph.sem("small")
        one_plus = ph.sem("one_plus")

        wqkv = dram["wqkv_t"].rearrange("(k p) n -> p k n", p=P)
        wo = dram["wo_t"].rearrange("(h p) n -> p h n", p=P)
        chunks = []
        for k in range(KC):
            for c in range(QKV // CH):
                at = slice(c * CH, (c + 1) * CH)
                chunks.append((wqkv[:, k, at], keep.wqkv_hi[:, k, at], keep.wqkv_lo[:, k, at]))
        for c in range(HEADS * D // CH):
            at = slice(c * CH, (c + 1) * CH)
            heads = slice(c * CH // D, (c + 1) * CH // D)
            chunks.append((wo[:, heads, :], keep.wo_hi[:, at], keep.wo_lo[:, at]))

        with nc.Block() as block:

            @block.sync
            def _(sp):
                gate = dram["gate_w"].rearrange("(k p) (m i) -> m p k i", p=P, i=P)
                up = dram["up_w"].rearrange("(k p) (m i) -> m p k i", p=P, i=P)
                down = dram["down_w"].rearrange("(m p) d -> m p d", p=P)
                for m in range(M):
                    three_w = raw8[:, m, :].rearrange("p (a k i) -> p a k i", a=3, k=KC)
                    sp.dma_start(three_w[:, 0], gate[m]).then_inc(ffn_loaded, 16)
                    sp.dma_start(three_w[:, 1], up[m]).then_inc(ffn_loaded, 16)
                    sp.dma_start(raw8[:, m, 2 * D:], down[m]).then_inc(ffn_loaded, 16)
                for n, (src, _, _) in enumerate(chunks):
                    if n >= RING:
                        sp.wait_ge(lo_done, n - RING + 1)
                    to = raw[:, n % RING, :]
                    if len(src.shape) == 3:
                        to = to.rearrange("p (h n) -> p h n", n=D)
                    sp.dma_start(to, src).then_inc(raw_loaded[n % RING], 16)
                sp.wait_ge(x_loaded, 16 * 8)
                sp.wait_ge(rows_loaded, 16 * 9)

            @block.scalar
            def _(act):
                x_in = dram["x"].rearrange("b (t p) d -> p (b t) d", p=P)
                n = SUB // 8
                act.dma_start(raw_scale[:, 0, :], dram["gate_s"]).then_inc(rows_loaded, 16)
                act.dma_start(raw_scale[:, 1, :], dram["up_s"]).then_inc(rows_loaded, 16)
                act.dma_start(keep.down_s[:, :], dram["down_s"].partition_broadcast(P)).then_inc(rows_loaded, 16)
                act.dma_start(wrow[:, 0, :], dram["qn"].partition_broadcast(P)).then_inc(rows_loaded, 16)
                act.dma_start(wrow[:, 1, :], dram["kn"].partition_broadcast(P)).then_inc(rows_loaded, 16)
                act.dma_start(rope_raw[:, 0], dram["cos"].rearrange("(t p) d -> p t d", p=P)).then_inc(rows_loaded, 16)
                act.dma_start(rope_raw[:, 1], dram["sin"].rearrange("(t p) d -> p t d", p=P)).then_inc(rows_loaded, 16)
                act.dma_start(keep.ident[:, :], dram["ident"]).then_inc(rows_loaded, 16)
                act.dma_start(keep.mask[:, :], dram["mask"]).then_inc(rows_loaded, 16)
                for s in range(8):
                    act.dma_start(keep.x[:, s * n:(s + 1) * n, :], x_in[:, s * n:(s + 1) * n, :]).then_inc(x_loaded, 16)
                for n, (_, hi, _) in enumerate(chunks):
                    act.wait_ge(raw_loaded[n % RING], 16 * (n // RING + 1))
                    act.activation(hi, raw[:, n % RING, :], ACT.Copy).then_inc(hi_done, 1)

            @block.gpsimd
            def _(pool):
                for m in range(M):
                    pool.wait_ge(rounded, m + 1)
                    if m >= 2:
                        pool.wait_ge(f8_ready, m - 1)
                    pool.tensor_scalar(over[:, m % 2, :], q8[:, m % 2, :], F8_OVER, 0.0, ALU.mult, ALU.mult).then_inc(over_ready, 1)

                for n, (_, hi, lo) in enumerate(chunks):
                    if n % 2:
                        pool.wait_ge(hi_done, n + 1)
                        pool.wait_ge(lo_done, n)
                        pool.tensor_tensor(lo, raw[:, n % RING, :], hi.bitcast(F32), ALU.subtract).then_inc(lo_done, 1)

            @block.vector
            def _(dve):
                dve.wait_ge(rows_loaded, 16 * 9)
                dve.tensor_scalar(keep.gate_half[:, :], raw_scale[:, 0, :], 0.5, None, ALU.mult).then_inc(small, 1)
                dve.scalar_tensor_tensor(keep.gate_up[:, :], raw_scale[:, 0, :], 0.5, raw_scale[:, 1, :], ALU.mult, ALU.mult).then_inc(small, 1)
                dve.tensor_scalar(keep.down_half[:, :], keep.down_s[:, :], 0.5, None, ALU.mult).then_inc(small, 1)
                dve.tensor_scalar(wrow[:, :, :], wrow[:, :, :], 1.0, None, ALU.add).then_inc(one_plus, 1)
                dve.wait_ge(one_plus, 1)
                for n in range(2):
                    w = wrow[:, n, :]
                    swapped = w.rearrange("p (s d) -> p s d", s=2)[:, ::-1, :]
                    for t in range(2):
                        dve.tensor_tensor(keep.rope[:, n, 0, t, :], rope_raw[:, 0, t, :], w, ALU.mult).then_inc(small, 1)
                        dve.tensor_tensor(keep.rope[:, n, 1, t, :].rearrange("p (s d) -> p s d", s=2),
                                          rope_raw[:, 1, t, :].rearrange("p (s d) -> p s d", s=2), swapped, ALU.mult).then_inc(small, 1)

                def low(n):
                    _, hi, lo = chunks[n]
                    dve.wait_ge(hi_done, n + 1)
                    if n:
                        dve.wait_ge(lo_done, n)
                    dve.tensor_tensor(lo, raw[:, n % RING, :], hi.bitcast(F32), ALU.subtract).then_inc(lo_done, 1)

                for m in range(M):
                    w, mg, q = raw8[:, m, :], magic[:, m % 2, :], q8[:, m % 2, :]
                    dve.wait_ge(ffn_loaded, 16 * 3 * M)
                    dve.tensor_scalar(mg.bitcast(I32), w.bitcast(I32), 0x7F800000, None, ALU.bitwise_and).then_inc(exponent, 1)
                    dve.wait_ge(exponent, m + 1)
                    dve.tensor_scalar(mg, mg, F8_MIN_NORMAL, F8_MAGIC, ALU.max, ALU.mult).then_inc(magic_ready, 1)
                    dve.wait_ge(magic_ready, m + 1)
                    dve.tensor_tensor(w, w, mg, ALU.add).then_inc(added, 1)
                    if m >= 1:
                        dve.wait_ge(over_ready, m)
                        dve.tensor_tensor(keep.w8[:, m - 1, :], q8[:, (m - 1) % 2, :], over[:, (m - 1) % 2, :], ALU.add).then_inc(f8_ready, 1)
                    dve.wait_ge(added, m + 1)
                    dve.tensor_tensor(q, w, mg, ALU.subtract).then_inc(rounded, 1)
                    dve.wait_ge(rounded, m + 1)
                dve.wait_ge(over_ready, M)
                dve.tensor_tensor(keep.w8[:, M - 1, :], q8[:, (M - 1) % 2, :], over[:, (M - 1) % 2, :], ALU.add).then_inc(f8_ready, 1)
                for n in range(0, len(chunks), 2):
                    low(n)


def ffn_phase(nc, semaphores, keep, prefix, out_dram=None):
    TILE = 512
    SUBS = TILE // P
    TILES = BATCH * T // TILE
    GU_AHEAD = 2
    with ExitStack() as stack:
        ph = Phase(nc, stack, semaphores, prefix)
        w8 = ph.sb("w8", [P, M, 3 * D], F32R)
        stats = ph.sb("stats", [P, SUBS, 6], F32)
        mv = ph.sb("mv", [P, SUBS, 2], F32)
        var = ph.sb("var", [P, SUBS], F32)
        rstd = ph.sb("rstd", [P, SUBS], F32)
        nmr = ph.sb("nmr", [P, SUBS], F32)
        power = ph.sb("power", [P, SUBS], F32)
        y = ph.sb("y", [P, SUBS, D], F32)
        yt_hi = ph.sb("yt_hi", [P, 2, KC, TILE], F32R)
        yt_lo = ph.sb("yt_lo", [P, 2, KC, TILE], F32R)
        th = ph.sb("th", [P, 2, TILE], F32)
        gated = ph.sb("gated", [P, 2, TILE], F32)
        h = ph.sb("h", [P, 2, TILE], F32)
        h_hi = ph.sb("h_hi", [P, 3, TILE], F32R)
        h_lo = ph.sb("h_lo", [P, 3, TILE], F32R)
        scaled = ph.sb("scaled", [P, 2, TILE], F32)

        gate = [ph.ps(f"gate{k}") for k in range(2)]
        up = [ph.ps(f"up{k}") for k in range(2)]
        turn = [ph.ps(f"turn{k}") for k in range(KC)]
        acc = [ph.ps(f"acc{k}") for k in range(2)]

        w8_ready = ph.sem("w8_ready")
        stats_done = ph.sem("stats_done")
        mv_ready = ph.sem("mv_ready")
        power_set = ph.sem("power_set")
        var_ready = ph.sem("var_ready")
        rstd_ready = ph.sem("rstd_ready")
        mr_ready = ph.sem("mr_ready")
        nmr_ready = ph.sem("nmr_ready")
        y_ready = ph.sem("y_ready")
        turned = ph.sem("turned")
        yt_hi_ready = ph.sem("yt_hi_ready")
        yt_ready = ph.sem("yt_ready")
        gate_ready = ph.sem("gate_ready")
        up_ready = ph.sem("up_ready")
        th_ready = ph.sem("th_ready")
        gate_used = ph.sem("gate_used")
        h_ready = ph.sem("h_ready")
        h_hi_ready = ph.sem("h_hi_ready")
        h_split = ph.sem("h_split")
        down_done = ph.sem("down_done")
        acc_used = ph.sem("acc_used")
        x_done = ph.sem("x_done")
        stored = ph.sem("stored")

        def wait(eng, sem, value):
            if not isinstance(value, int) or value > 0:
                eng.wait_ge(sem, value)

        def pairs(eng, tile):
            tile(0, 0, 0, 2)
            tile(1, 1, 1, 2)
            with eng.Fori(1, TILES // 2 - 1) as pair:
                tile(2 * pair, 0, 2, 2)
                tile(2 * pair + 1, 1, 2, 2)
            tile(TILES - 2, 0, 2, 1)
            tile(TILES - 1, 1, 2, 0)

        def x_of(t):
            return keep.x[:, bass.ds(t * SUBS, SUBS), :]

        with nc.Block() as block:

            @block.tensor
            def _(pe):
                def turn_y(t):
                    pe.wait_ge(y_ready, SUBS * (t + 1))
                    wait(pe, yt_ready, KC * t)
                    for k in range(KC):
                        for s in range(SUBS):
                            last = pe.transpose(turn[k][:, s * P:(s + 1) * P], y[:, s, k * P:(k + 1) * P], keep.ident[:, :])
                        last.then_inc(turned, 1)

                def gate_up(t, parity, m):
                    step = t * M + m
                    if m == 0:
                        pe.wait_ge(yt_ready, KC * (t + 1))
                    wait(pe, gate_used, step - 1)
                    for a, (bank, ready) in enumerate(((gate[m % 2], gate_ready), (up[m % 2], up_ready))):
                        if a:
                            wait(pe, h_ready, step - 1)
                        parts = []
                        for k in range(KC):
                            w = w8[:, m, a * D + k * P:a * D + (k + 1) * P]
                            parts += [(w, yt_hi[:, parity, k, :]), (w, yt_lo[:, parity, k, :])]
                        product(pe, bank[:, :], parts).then_inc(ready, 1)

                def down(t, m):
                    step = t * M + m
                    pe.wait_ge(h_split, step + 1)
                    if m == 0:
                        wait(pe, acc_used, 2 * t)
                    w = w8[:, m, 2 * D:]
                    for s in range(SUBS):
                        at = slice(s * P, (s + 1) * P)
                        out = acc[s // 2][:, (s % 2) * D:(s % 2 + 1) * D]
                        last = product(pe, out, [(h_hi[:, m % 3, at], w), (h_lo[:, m % 3, at], w)],
                                       start=(m == 0 and s % 2 == 0), stop=(m == M - 1))
                    last.then_inc(down_done, 1)

                def tile(t, parity, before, after):
                    for m in range(M):
                        if m + GU_AHEAD < M:
                            gate_up(t, parity, m + GU_AHEAD)
                        elif after:
                            gate_up(t + 1, 1 - parity, m + GU_AHEAD - M)
                        down(t, m)
                        if m == 1 and after:
                            turn_y(t + 1)

                turn_y(0)
                pe.wait_ge(w8_ready, 2)
                gate_up(0, 0, 0)
                gate_up(0, 0, 1)
                pairs(pe, tile)

            @block.scalar
            def _(act):
                def normalise(t, subs):
                    act.wait_ge(nmr_ready, t + 1)
                    wait(act, turned, KC * t)
                    for s in subs:
                        act.activation(y[:, s, :], keep.x[:, bass.ds(t * SUBS + s, 1), :].rearrange("p a d -> p (a d)"), ACT.Identity,
                                       bias=nmr[:, s:s + 1], scale=rstd[:, s:s + 1]).then_inc(y_ready, 1)

                def yt_high(t, parity):
                    for k in range(KC):
                        act.wait_ge(turned, KC * t + k + 1)
                        if k == 0:
                            wait(act, up_ready, M * (t - 1))
                        act.activation(yt_hi[:, parity, k, :], turn[k][:, :], ACT.Copy).then_inc(yt_hi_ready, 1)

                def tanh(t, m):
                    step = t * M + m
                    act.wait_ge(gate_ready, step + 1)
                    wait(act, gate_used, step - 1)
                    act.activation(th[:, m % 2, :], gate[m % 2][:, :], ACT.Tanh, scale=keep.gate_half[:, m:m + 1]).then_inc(th_ready, 1)

                def tile(t, parity, before, after):
                    for m in range(M):
                        step = t * M + m
                        if m + 1 < M:
                            tanh(t, m + 1)
                        elif after:
                            tanh(t + 1, 0)
                        act.wait_ge(h_ready, step + 1)
                        wait(act, down_done, step - 2)
                        act.activation(h_hi[:, m % 3, :], h[:, m % 2, :], ACT.Copy).then_inc(h_hi_ready, 1)
                        if m == 2 and after:
                            yt_high(t + 1, 1 - parity)
                        if m in (3, 4) and after == 2:
                            normalise(t + 2, range(2 * (m - 3), 2 * (m - 2)))

                act.activation(w8[:, 0:M // 2, :], keep.w8[:, 0:M // 2, :], ACT.Copy).then_inc(w8_ready, 1)
                normalise(0, range(SUBS))
                yt_high(0, 0)
                normalise(1, range(SUBS))
                tanh(0, 0)
                pairs(act, tile)

            @block.vector
            def _(dve):
                def statistics(t):
                    wait(dve, nmr_ready, t)
                    for s in range(SUBS):
                        dve.bn_stats(stats[:, s, :], keep.x[:, bass.ds(t * SUBS + s, 1), :].rearrange("p a d -> p (a d)")).then_inc(stats_done, 1)
                    for s in range(SUBS):
                        dve.wait_ge(stats_done, SUBS * t + s + 1)
                        stand(dve)
                        dve.bn_aggr(mv[:, s, :], stats[:, s, :]).then_inc(mv_ready, 1)

                def yt_low(t, parity):
                    for k in range(KC):
                        dve.wait_ge(yt_hi_ready, KC * t + k + 1)
                        dve.tensor_tensor(yt_lo[:, parity, k, :], turn[k][:, :], yt_hi[:, parity, k, :].bitcast(F32), ALU.subtract).then_inc(yt_ready, 1)

                def scale_sums(t):
                    dve.wait_ge(down_done, M * (t + 1))
                    wait(dve, x_done, 2 * t)
                    for k in range(2):
                        scale = keep.down_half[:, None, :].broadcast_to([P, 2, D])
                        dve.tensor_tensor(scaled[:, k, :].rearrange("p (s d) -> p s d", d=D), acc[k][:, :].rearrange("p (s d) -> p s d", d=D),
                                          scale, ALU.mult).then_inc(acc_used, 1)

                def tile(t, parity, before, after):
                    for m in range(M):
                        step = t * M + m
                        dve.wait_ge(th_ready, step + 1)
                        dve.scalar_tensor_tensor(gated[:, m % 2, :], th[:, m % 2, :], 1.0, gate[m % 2][:, :], ALU.add, ALU.mult).then_inc(gate_used, 1)
                        dve.wait_ge(up_ready, step + 1)
                        dve.wait_ge(gate_used, step + 1)
                        wait(dve, h_split, step - 1)
                        dve.scalar_tensor_tensor(h[:, m % 2, :], up[m % 2][:, :], keep.gate_up[:, m:m + 1], gated[:, m % 2, :], ALU.mult, ALU.mult).then_inc(h_ready, 1)
                        if m == 0 and before:
                            scale_sums(t - 1)
                        if m == 2 and after:
                            yt_low(t + 1, 1 - parity)
                        if m == 1 and after == 2:
                            statistics(t + 2)

                dve.tensor_copy(w8[:, M // 2:, :], keep.w8[:, M // 2:, :]).then_inc(w8_ready, 1)
                statistics(0)
                statistics(1)
                yt_low(0, 0)
                pairs(dve, tile)
                scale_sums(TILES - 1)

            @block.gpsimd
            def _(pool):
                def rstd_of(t):
                    pool.wait_ge(mv_ready, SUBS * (t + 1))
                    wait(pool, y_ready, SUBS * t)
                    stand(pool)
                    pool.tensor_scalar(var[:, :], mv[:, :, 1], 1.0, LN_EPS, ALU.mult, ALU.add).then_inc(var_ready, 1)
                    pool.wait_ge(var_ready, t + 1)
                    pool.tensor_tensor(rstd[:, :], var[:, :], power[:, :], ALU.pow).then_inc(rstd_ready, 1)
                    pool.wait_ge(rstd_ready, t + 1)
                    pool.tensor_tensor(nmr[:, :], mv[:, :, 0], rstd[:, :], ALU.mult).then_inc(mr_ready, 1)
                    pool.wait_ge(mr_ready, t + 1)
                    stand(pool)
                    pool.tensor_scalar(nmr[:, :], nmr[:, :], -1.0, 1.0, ALU.mult, ALU.mult).then_inc(nmr_ready, 1)

                def add_to_x(t, k):
                    pool.wait_ge(acc_used, 2 * t + k + 1)
                    at = keep.x[:, bass.ds(t * SUBS + 2 * k, 2), :].rearrange("p s d -> p (s d)")
                    pool.tensor_tensor(at, at, scaled[:, k, :], ALU.add).then_inc(x_done, 1)

                def tile(t, parity, before, after):
                    for m in range(M):
                        step = t * M + m
                        pool.wait_ge(h_hi_ready, step + 1)
                        pool.tensor_tensor(h_lo[:, m % 3, :], h[:, m % 2, :], h_hi[:, m % 3, :].bitcast(F32), ALU.subtract).then_inc(h_split, 1)
                        if m in (0, 1) and before:
                            add_to_x(t - 1, m)
                        if m == 2 and after == 2:
                            rstd_of(t + 2)

                pool.memset(power[:, :], -0.5).then_inc(power_set, 1)
                pool.wait_ge(power_set, 1)
                rstd_of(0)
                rstd_of(1)
                pairs(pool, tile)
                add_to_x(TILES - 1, 0)
                add_to_x(TILES - 1, 1)

            @block.sync
            def _(sp):
                if out_dram is not None:
                    view = out_dram.rearrange("b (t p) d -> p (b t) d", p=P)
                    with sp.Fori(0, TILES) as t:
                        sp.wait_ge(x_done, 2 * t + 2)
                        sp.dma_start(view[:, bass.ds(t * SUBS, SUBS), :], x_of(t)).then_inc(stored, 16)
                    sp.wait_ge(stored, 16 * TILES)


RING = 7


def fills_of_batch(first, last):
    fills = []
    for g in range(KV):
        ahead = g < KV - 1 or not last
        fills += [("S", g, h) for h in range(GROUP)]
        if g == KV - 1 and ahead:
            fills += [("K", g, 0), ("K", g, 1)]
        if ahead:
            fills += [("J", g, 0), ("J", g, 1)]
        if g > 0 or not first:
            fills += [("C", g, 0), ("C", g, 1)]
        if g == 0:
            fills += [("V", g, 0), ("V", g, 1)]
        fills += [("P", g, h) for h in range(GROUP)]
        if ahead:
            fills += [("Q", g, 0), ("Q", g, 1)]
        if g == KV - 2 and not last:
            fills += [("Y", g, 0)]
        if g == KV - 1 and ahead:
            fills += [("T", g, 0), ("T", g, 1)]
    return fills


BEFORE = [("Y", KV - 2, 0)] + [(what, KV - 1, t) for what in "KJTQ" for t in range(2)]
AFTER = [("C", 0, 0), ("C", 0, 1)]
FIRST, STEADY, LAST = fills_of_batch(True, False), fills_of_batch(False, False), fills_of_batch(False, True)
assert (len(BEFORE) + len(FIRST)) % RING == 0 and len(STEADY) % RING == 0


class Fills:

    def __init__(self, b):
        self.b = b
        at = b if isinstance(b, int) else 1
        self.own = {-1: BEFORE, 0: FIRST, BATCH - 1: LAST, BATCH: AFTER}.get(at, STEADY)
        self.former = {-1: [], 0: BEFORE, 1: FIRST, BATCH: LAST}.get(at, STEADY)
        self.start = {0: len(BEFORE), BATCH: len(LAST)}.get(at, 0)

    def bank(self, what, g, part):
        return (self.start + self.own.index((what, g, part))) % RING

    def contents_before(self, what, g, part):
        n = self.own.index((what, g, part)) - RING
        if n >= 0:
            return self.own[n], self.b
        return (self.former[n], self.b - 1) if self.former else None


def attention_phase(nc, semaphores, keep):
    QB = T // P
    SPAN = [P, P + WINDOW]
    SPANS = sum(SPAN)
    BLOCKS = 3
    HW = GROUP * P
    K_AT, V_AT = HEADS * DH, (HEADS + KV) * DH
    with ExitStack() as stack:
        ph = Phase(nc, stack, semaphores, "a_")
        stats = ph.sb("stats", [P, QB, 6], F32)
        mv = ph.sb("mv", [P, QB, 2], F32)
        var = ph.sb("var", [P, QB], F32)
        rstd = ph.sb("rstd", [P, QB], F32)
        nmr = ph.sb("nmr", [P, QB], F32)
        power = ph.sb("power", [P, QB, GROUP], F32)
        y = ph.sb("y", [P, QB, D], F32)
        yt_hi = ph.sb("yt_hi", [P, KC, T], F32R)
        yt_lo = ph.sb("yt_lo", [P, KC, T], F32R)
        q_cos = ph.sb("q_cos", [P, QB, HW], F32)
        k_cos = ph.sb("k_cos", [P, QB, HW], F32)
        by_sin = ph.sb("by_sin", [P, QB, HW], F32)
        squares = ph.sb("squares", [P, QB, HW], BF16)
        q_ss = ph.sb("q_ss", [P, QB, GROUP], F32)
        k_ss = ph.sb("k_ss", [P, QB, KV], F32)
        q_ms = ph.sb("q_ms", [P, QB, GROUP], F32)
        k_ms = ph.sb("k_ms", [P, QB, KV], F32)
        q_rs = ph.sb("q_rs", [P, 2, QB, GROUP], F32)
        k_rs = ph.sb("k_rs", [P, QB, KV], F32)
        qt_hi = ph.sb("qt_hi", [P, QB, HW], F32R)
        qt_lo = ph.sb("qt_lo", [P, QB, HW], F32R)
        kt_hi = ph.sb("kt_hi", [P, KV, T], F32R)
        kt_lo = ph.sb("kt_lo", [P, KV, T], F32R)
        v_hi = ph.sb("v_hi", [P, QB, HW], F32R)
        v_lo = ph.sb("v_lo", [P, QB, HW], F32R)
        masked = ph.sb("masked", [P, GROUP, SPANS], F32)
        top = ph.sb("top", [P, GROUP, QB], F32)
        minus_top = ph.sb("minus_top", [P, GROUP, QB], F32)
        prob = ph.sb("prob", [P, GROUP, BLOCKS * P], F32)
        total = ph.sb("total", [P, GROUP, QB], F32)
        inverse = ph.sb("inverse", [P, GROUP, QB], F32)
        pt_hi = ph.sb("pt_hi", [P, BLOCKS, HW], F32R)
        pt_lo = ph.sb("pt_lo", [P, BLOCKS, HW], F32R)
        ctx_hi = ph.sb("ctx_hi", [P, QB, HW], F32R)
        ctx_lo = ph.sb("ctx_lo", [P, QB, HW], F32R)

        ring = [ph.ps(f"ring{k}") for k in range(RING)]
        out = ph.ps("out")

        stats_done = ph.sem("stats_done")
        mv_ready = ph.sem("mv_ready")
        set_up = ph.sem("set_up")
        var_ready = ph.sem("var_ready")
        rstd_ready = ph.sem("rstd_ready")
        mr_ready = ph.sem("mr_ready")
        nmr_ready = ph.sem("nmr_ready")
        y_ready = ph.sem("y_ready")
        y_turned = ph.sem("y_turned")
        yt_hi_ready = ph.sem("yt_hi_ready")
        yt_ready = ph.sem("yt_ready")
        k_projected = ph.sem("k_projected")
        k_cos_done = ph.sem("k_cos_done")
        k_sin_done = ph.sem("k_sin_done")
        k_squared = ph.sem("k_squared")
        k_added = ph.sem("k_added")
        k_ms_ready = ph.sem("k_ms_ready")
        k_rs_ready = ph.sem("k_rs_ready")
        k_normed = ph.sem("k_normed")
        k_turned = ph.sem("k_turned")
        kt_hi_ready = ph.sem("kt_hi_ready")
        kt_ready = ph.sem("kt_ready")
        v_projected = ph.sem("v_projected")
        v_hi_ready = ph.sem("v_hi_ready")
        v_ready = ph.sem("v_ready")
        q_projected = ph.sem("q_projected")
        q_cos_done = ph.sem("q_cos_done")
        q_sin_done = ph.sem("q_sin_done")
        q_squared = ph.sem("q_squared")
        q_added = ph.sem("q_added")
        q_ms_ready = ph.sem("q_ms_ready")
        q_rs_ready = ph.sem("q_rs_ready")
        q_turned = ph.sem("q_turned")
        qt_hi_ready = ph.sem("qt_hi_ready")
        qt_ready = ph.sem("qt_ready")
        scored = ph.sem("scored")
        top_ready = ph.sem("top_ready")
        bias_ready = ph.sem("bias_ready")
        exp_done = ph.sem("exp_done")
        inverse_ready = ph.sem("inverse_ready")
        prob_ready = ph.sem("prob_ready")
        p_turned = ph.sem("p_turned")
        pt_hi_ready = ph.sem("pt_hi_ready")
        pt_ready = ph.sem("pt_ready")
        ctx_summed = ph.sem("ctx_summed")
        ctx_hi_ready = ph.sem("ctx_hi_ready")
        ctx_ready = ph.sem("ctx_ready")
        projected = ph.sem("projected")
        out_used = ph.sem("out_used")

        def wait(eng, sem, value):
            if not isinstance(value, int) or value > 0:
                eng.wait_ge(sem, value)

        def batches(eng, batch):
            batch(0, True, False)
            with eng.Fori(1, BATCH - 1) as b:
                batch(b, False, False)
            batch(BATCH - 1, False, True)

        def x_sub(b, t):
            return keep.x[:, bass.ds(b * QB + t, 1), :].rearrange("p a d -> p (a d)")

        def by_head(ap):
            return ap.rearrange("p (h d) -> p h d", h=GROUP)

        def halves(ap):
            return ap.rearrange("p (h s d) -> p h s d", h=GROUP, s=2)

        with nc.Block() as block:

            @block.tensor
            def _(pe):
                readers = {
                    "S": lambda b, g, h: (top_ready, QB * (GROUP * (KV * b + g) + h + 1)),
                    "J": lambda b, g, t: (q_squared, GROUP * (QB * (KV * b + g + 1) + t + 1)),
                    "K": lambda b, g, t: (k_squared, GROUP * (QB * (b + 1) + t + 1)),
                    "V": lambda b, g, t: (v_ready, QB * b + t + 1),
                    "C": lambda b, g, t: (ctx_ready, QB * (KV * b + g - 1) + t + 1),
                    "P": lambda b, g, h: (pt_ready, GROUP * (KV * b + g) + h + 1),
                    "Y": lambda b, g, _: (yt_ready, b + 2),
                    "T": lambda b, g, t: (kt_ready, QB * (b + 1) + t + 1),
                    "Q": lambda b, g, t: (qt_ready, QB * (KV * b + g + 1) + t + 1),
                }

                def begin(f, what, g, part):
                    before = f.contents_before(what, g, part)
                    if before:
                        (what0, g0, part0), b0 = before
                        pe.wait_ge(*readers[what0](b0, g0, part0))
                    return ring[f.bank(what, g, part)]

                def turn_y(f):
                    b = f.b + 1
                    bank = begin(f, "Y", KV - 2, 0)
                    pe.wait_ge(y_ready, QB * (b + 1))
                    for k in range(KC):
                        for t in range(QB):
                            last = pe.transpose(bank[:, k * T + t * P:k * T + (t + 1) * P], y[:, t, k * P:(k + 1) * P], keep.ident[:, :])
                    last.then_inc(y_turned, 1)

                def project(f, what, g, b, at, done):
                    for t in range(QB):
                        bank = begin(f, what, g, t)
                        pe.wait_ge(yt_ready, b + 1)
                        parts = []
                        for k in range(KC):
                            tok = slice(t * P, (t + 1) * P)
                            parts += three(yt_hi[:, k, tok], yt_lo[:, k, tok], keep.wqkv_hi[:, k, at:at + HW], keep.wqkv_lo[:, k, at:at + HW])
                        product(pe, bank[:, :], parts).then_inc(done, 1)

                def turn_heads(bank, src, done):
                    for h in range(GROUP):
                        at = slice(h * P, (h + 1) * P)
                        last = pe.transpose(bank[:, at], src[:, at], keep.ident[:, :])
                    last.then_inc(done, 1)

                def turn_q(f, g):
                    for t in range(QB):
                        bank = begin(f, "Q", g, t)
                        pe.wait_ge(q_added, QB * (KV * f.b + g + 1) + t + 1)
                        turn_heads(bank, q_cos[:, t, :], q_turned)

                def turn_k(f):
                    for t in range(QB):
                        bank = begin(f, "T", KV - 1, t)
                        pe.wait_ge(k_normed, QB * (f.b + 1) + t + 1)
                        turn_heads(bank, k_cos[:, t, :], k_turned)

                def scores(f, g, h):
                    bank = begin(f, "S", g, h)
                    if h == 0:
                        pe.wait_ge(qt_ready, QB * (KV * f.b + g + 1))
                        pe.wait_ge(kt_ready, QB * (f.b + 1))
                    at = slice(h * P, (h + 1) * P)
                    first = 0
                    for t in range(QB):
                        keys = slice((t + 1) * P - SPAN[t], (t + 1) * P)
                        last = product(pe, bank[:, first:first + SPAN[t]],
                                       three(qt_hi[:, t, at], qt_lo[:, t, at], kt_hi[:, g, keys], kt_lo[:, g, keys]))
                        first += SPAN[t]
                    last.then_inc(scored, 1)

                def turn_probs(f, g, h):
                    bank = begin(f, "P", g, h)
                    pe.wait_ge(prob_ready, QB * (GROUP * (KV * f.b + g) + h + 1))
                    for k in range(BLOCKS):
                        last = pe.transpose(bank[:, k * P:(k + 1) * P], prob[:, h, k * P:(k + 1) * P], keep.ident[:, :])
                    last.then_inc(p_turned, 1)

                def context(f, g):
                    n = KV * f.b + g - 1
                    v_at = slice((g - 1) % KV * DH, ((g - 1) % KV + 1) * DH)
                    pe.wait_ge(pt_ready, GROUP * (n + 1))
                    pe.wait_ge(v_ready, QB * (f.b + 1) if g else QB * f.b)
                    for t in range(QB):
                        bank = begin(f, "C", g, t)
                        parts = []
                        for k in range(t + 1):
                            parts += three(v_hi[:, k, v_at], v_lo[:, k, v_at], pt_hi[:, t + k, :], pt_lo[:, t + k, :])
                        product(pe, bank[:, :], parts).then_inc(ctx_summed, 1)

                def out_projection(b, g, t):
                    n = KV * b + g - 1
                    g = (g - 1) % KV
                    pe.wait_ge(ctx_ready, QB * n + t + 1)
                    if g == 0 and t == 0:
                        wait(pe, out_used, b)
                    for h in range(GROUP):
                        at = slice(h * P, (h + 1) * P)
                        w = slice((g * GROUP + h) * D, (g * GROUP + h + 1) * D)
                        last = product(pe, out[:, t * D:(t + 1) * D],
                                       three(ctx_hi[:, t, at], ctx_lo[:, t, at], keep.wo_hi[:, w], keep.wo_lo[:, w]),
                                       start=(g == 0 and t == 0 and h == 0), stop=(g == KV - 1 and h == GROUP - 1))
                    last.then_inc(projected, 1)

                def batch(b, first, last):
                    f = Fills(b)
                    for g in range(KV):
                        ahead = g < KV - 1 or not last
                        behind = g > 0 or not first
                        for h in range(GROUP):
                            scores(f, g, h)
                        if g == KV - 1 and ahead:
                            project(f, "K", g, b + 1, K_AT, k_projected)
                            project(f, "J", g, b + 1, 0, q_projected)
                        elif ahead:
                            project(f, "J", g, b, (g + 1) * HW, q_projected)
                        if behind:
                            context(f, g)
                        if g == 0:
                            project(f, "V", g, b, V_AT, v_projected)
                        for h in range(GROUP):
                            turn_probs(f, g, h)
                        if ahead:
                            turn_q(f, g)
                        if g == KV - 2 and not last:
                            turn_y(f)
                        if g == KV - 1 and ahead:
                            turn_k(f)
                        if behind:
                            out_projection(b, g, 0)
                            out_projection(b, g, 1)

                f = Fills(-1)
                pe.wait_ge(set_up, 2)
                turn_y(f)
                project(f, "K", KV - 1, 0, K_AT, k_projected)
                project(f, "J", KV - 1, 0, 0, q_projected)
                turn_k(f)
                turn_q(f, KV - 1)
                batches(pe, batch)
                context(Fills(BATCH), 0)
                out_projection(BATCH, 0, 0)
                out_projection(BATCH, 0, 1)

            @block.scalar
            def _(act):
                def normalise(b):
                    act.wait_ge(nmr_ready, b + 1)
                    wait(act, y_turned, b)
                    for t in range(QB):
                        act.activation(y[:, t, :], x_sub(b, t), ACT.Identity, bias=nmr[:, t:t + 1], scale=rstd[:, t:t + 1]).then_inc(y_ready, 1)

                def squares_of(bank, t, ss, done):
                    for h in range(GROUP):
                        at = slice(h * P, (h + 1) * P)
                        act.activation(squares[:, t, at], bank[:, at], ACT.Square, accum_out=ss[:, t, h:h + 1]).then_inc(done, 1)

                def square_k(f):
                    b = f.b + 1
                    wait(act, k_rs_ready, b)
                    wait(act, q_squared, GROUP * QB * KV * b)
                    for t in range(QB):
                        act.wait_ge(k_sin_done, QB * b + t + 1)
                        squares_of(ring[f.bank("K", KV - 1, t)], t, k_ss, k_squared)

                def square_q(f, g):
                    n = KV * f.b + g + 1
                    wait(act, q_rs_ready, n)
                    wait(act, q_squared, GROUP * QB * n)
                    if g == KV - 1:
                        act.wait_ge(k_squared, GROUP * QB * (f.b + 2))
                    for t in range(QB):
                        act.wait_ge(q_sin_done, QB * n + t + 1)
                        squares_of(ring[f.bank("J", g, t)], t, q_ss, q_squared)

                def exponentials(b, g, h):
                    n = GROUP * (KV * b + g) + h
                    act.wait_ge(bias_ready, n + 1)
                    wait(act, p_turned, n - GROUP + 1)
                    first = 0
                    for t in range(QB):
                        to = BLOCKS * P if t else P
                        act.activation(prob[:, h, to - SPAN[t]:to], masked[:, h, first:first + SPAN[t]], ACT.Exp,
                                       bias=minus_top[:, h, t:t + 1], scale=q_rs[:, g % 2, t, h:h + 1],
                                       accum_out=total[:, h, t:t + 1]).then_inc(exp_done, 1)
                        first += SPAN[t]

                def high_y(f):
                    b = f.b + 1
                    act.wait_ge(y_turned, b + 1)
                    wait(act, q_projected, QB * KV * b)
                    act.activation(yt_hi[:, :, :], ring[f.bank("Y", KV - 2, 0)][:, :].rearrange("p (k t) -> p k t", k=KC), ACT.Copy).then_inc(yt_hi_ready, 1)

                def high_k(f):
                    b = f.b + 1
                    wait(act, scored, GROUP * KV * b)
                    for t in range(QB):
                        act.wait_ge(k_turned, QB * b + t + 1)
                        act.activation(kt_hi[:, :, t * P:(t + 1) * P], by_head(ring[f.bank("T", KV - 1, t)][:, :]), ACT.Copy).then_inc(kt_hi_ready, 1)

                def high_v(f):
                    wait(act, ctx_summed, QB * KV * f.b)
                    for t in range(QB):
                        act.wait_ge(v_projected, QB * f.b + t + 1)
                        act.activation(v_hi[:, t, :], ring[f.bank("V", 0, t)][:, :], ACT.Copy).then_inc(v_hi_ready, 1)

                def high_q(f, g):
                    n = KV * f.b + g + 1
                    wait(act, scored, GROUP * n)
                    for t in range(QB):
                        act.wait_ge(q_turned, QB * n + t + 1)
                        act.activation(qt_hi[:, t, :], ring[f.bank("Q", g, t)][:, :], ACT.Copy).then_inc(qt_hi_ready, 1)

                def high_p(f, g, h):
                    n = KV * f.b + g
                    act.wait_ge(p_turned, GROUP * n + h + 1)
                    wait(act, ctx_summed, QB * n)
                    act.activation(pt_hi[:, :, h * P:(h + 1) * P],
                                   ring[f.bank("P", g, h)][:, 0:BLOCKS * P].rearrange("p (k q) -> p k q", k=BLOCKS), ACT.Copy).then_inc(pt_hi_ready, 1)

                def high_c(f, g):
                    n = KV * f.b + g - 1
                    for t in range(QB):
                        act.wait_ge(ctx_summed, QB * n + t + 1)
                        wait(act, projected, QB * (n - 1) + t + 1)
                        act.activation(ctx_hi[:, t, :], ring[f.bank("C", g, t)][:, :], ACT.Copy).then_inc(ctx_hi_ready, 1)

                def batch(b, first, last):
                    f = Fills(b)
                    for g in range(KV):
                        ahead = g < KV - 1 or not last
                        for h in range(GROUP):
                            exponentials(b, g, h)
                        if g == KV - 1 and ahead:
                            square_k(f)
                        if ahead:
                            square_q(f, g)
                        if g > 0 or not first:
                            high_c(f, g)
                        if g == 0:
                            high_v(f)
                        if g == 1 and not last:
                            normalise(b + 1)
                        for h in range(GROUP):
                            high_p(f, g, h)
                        if ahead:
                            high_q(f, g)
                        if g == KV - 2 and not last:
                            high_y(f)
                        if g == KV - 1 and ahead:
                            high_k(f)

                f = Fills(-1)
                normalise(0)
                high_y(f)
                square_k(f)
                square_q(f, KV - 1)
                high_k(f)
                high_q(f, KV - 1)
                batches(act, batch)
                high_c(Fills(BATCH), 0)

            @block.vector
            def _(dve):
                def statistics(b):
                    wait(dve, nmr_ready, b)
                    for t in range(QB):
                        dve.bn_stats(stats[:, t, :], x_sub(b, t)).then_inc(stats_done, 1)
                    for t in range(QB):
                        dve.wait_ge(stats_done, QB * b + t + 1)
                        stand(dve)
                        dve.bn_aggr(mv[:, t, :], stats[:, t, :]).then_inc(mv_ready, 1)

                def rope(bank, table, t, by_cos, cos_done, sin_done):
                    cos = keep.rope[:, table, 0, t, :]
                    sin = keep.rope[:, table, 1, t, :].rearrange("p (s d) -> p s d", s=2)
                    dve.tensor_tensor(by_head(by_cos[:, t, :]), by_head(bank[:, :]), cos[:, None, :].broadcast_to([P, GROUP, P]), ALU.mult).then_inc(cos_done, 1)
                    dve.tensor_tensor(halves(by_sin[:, t, :]), halves(bank[:, :])[:, :, ::-1, :],
                                      sin[:, None, :, :].broadcast_to([P, GROUP, 2, P // 2]), ALU.mult).then_inc(sin_done, 1)

                def rope_k(f):
                    b = f.b + 1
                    for t in range(QB):
                        dve.wait_ge(k_projected, QB * b + t + 1)
                        wait(dve, k_turned, QB * (b - 1) + t + 1)
                        wait(dve, q_added, QB * (KV * b - 1) + t + 1)
                        rope(ring[f.bank("K", KV - 1, t)], 1, t, k_cos, k_cos_done, k_sin_done)

                def rope_q(f, g, t):
                    n = KV * f.b + g + 1
                    dve.wait_ge(q_projected, QB * n + t + 1)
                    wait(dve, q_turned, QB * (n - 1) + t + 1)
                    if g == KV - 1:
                        dve.wait_ge(k_added, QB * (f.b + 1) + t + 1)
                    rope(ring[f.bank("J", g, t)], 0, t, q_cos, q_cos_done, q_sin_done)

                def maxima(f, g, h):
                    n = GROUP * (KV * f.b + g) + h
                    bank = ring[f.bank("S", g, h)]
                    dve.wait_ge(scored, n + 1)
                    wait(dve, exp_done, QB * (n - GROUP + 1))
                    stand(dve)
                    first = 0
                    for t in range(QB):
                        at = slice(first, first + SPAN[t])
                        dve.tensor_tensor_reduce(masked[:, h, at], bank[:, at], keep.mask[:, at], 1.0, -3e38, ALU.add, ALU.max,
                                                 top[:, h, t:t + 1]).then_inc(top_ready, 1)
                        first += SPAN[t]
                    dve.wait_ge(top_ready, QB * (n + 1))
                    if h == 0:
                        dve.wait_ge(q_rs_ready, KV * f.b + g + 1)
                    dve.scalar_tensor_tensor(minus_top[:, h, :], top[:, h, :], -1.0, q_rs[:, g % 2, :, h], ALU.mult, ALU.mult).then_inc(bias_ready, 1)

                def invert(b, g, h):
                    n = GROUP * (KV * b + g) + h
                    dve.wait_ge(exp_done, QB * (n + 1))
                    dve.reciprocal(inverse[:, h, :], total[:, h, :]).then_inc(inverse_ready, 1)

                def low(dst, hi, src, done):
                    dve.tensor_tensor(dst, src, hi.bitcast(F32), ALU.subtract).then_inc(done, 1)

                def low_y(f):
                    dve.wait_ge(yt_hi_ready, f.b + 2)
                    low(yt_lo[:, :, :], yt_hi[:, :, :], ring[f.bank("Y", KV - 2, 0)][:, :].rearrange("p (k t) -> p k t", k=KC), yt_ready)

                def low_k(f):
                    for t in range(QB):
                        at = slice(t * P, (t + 1) * P)
                        dve.wait_ge(kt_hi_ready, QB * (f.b + 1) + t + 1)
                        low(kt_lo[:, :, at], kt_hi[:, :, at], by_head(ring[f.bank("T", KV - 1, t)][:, :]), kt_ready)

                def low_v(f):
                    for t in range(QB):
                        dve.wait_ge(v_hi_ready, QB * f.b + t + 1)
                        low(v_lo[:, t, :], v_hi[:, t, :], ring[f.bank("V", 0, t)][:, :], v_ready)

                def low_q(f, g):
                    n = KV * f.b + g + 1
                    for t in range(QB):
                        dve.wait_ge(qt_hi_ready, QB * n + t + 1)
                        low(qt_lo[:, t, :], qt_hi[:, t, :], ring[f.bank("Q", g, t)][:, :], qt_ready)

                def low_p(f, g, h):
                    at = slice(h * P, (h + 1) * P)
                    dve.wait_ge(pt_hi_ready, GROUP * (KV * f.b + g) + h + 1)
                    low(pt_lo[:, :, at], pt_hi[:, :, at], ring[f.bank("P", g, h)][:, 0:BLOCKS * P].rearrange("p (k q) -> p k q", k=BLOCKS), pt_ready)

                def low_c(f, g):
                    n = KV * f.b + g - 1
                    for t in range(QB):
                        dve.wait_ge(ctx_hi_ready, QB * n + t + 1)
                        low(ctx_lo[:, t, :], ctx_hi[:, t, :], ring[f.bank("C", g, t)][:, :], ctx_ready)

                def add_output(b):
                    dve.wait_ge(projected, QB * KV * (b + 1))
                    at = keep.x[:, bass.ds(b * QB, QB), :].rearrange("p t d -> p (t d)")
                    dve.tensor_tensor(at, out[:, :], at, ALU.add).then_inc(out_used, 1)

                def batch(b, first, last):
                    f = Fills(b)
                    for g in range(KV):
                        ahead = g < KV - 1 or not last
                        behind = g > 0 or not first
                        for h in range(GROUP):
                            maxima(f, g, h)
                        invert(b, g, 0)
                        invert(b, g, 1)
                        if g == KV - 1 and ahead:
                            rope_k(f)
                        if ahead:
                            rope_q(f, g, 0)
                        invert(b, g, 2)
                        invert(b, g, 3)
                        if ahead:
                            rope_q(f, g, 1)
                        if g == 1 and not first:
                            add_output(b - 1)
                        if behind:
                            low_c(f, g)
                        if g == 0:
                            low_v(f)
                        for h in range(GROUP):
                            low_p(f, g, h)
                        if ahead:
                            low_q(f, g)
                        if g == KV - 2 and not last:
                            low_y(f)
                        if g == KV - 1 and ahead:
                            low_k(f)
                        if g == 0 and not last:
                            statistics(b + 1)

                f = Fills(-1)
                statistics(0)
                low_y(f)
                rope_k(f)
                rope_q(f, KV - 1, 0)
                rope_q(f, KV - 1, 1)
                low_k(f)
                low_q(f, KV - 1)
                batches(dve, batch)
                low_c(Fills(BATCH), 0)
                add_output(BATCH - 1)
                dve.wait_ge(out_used, BATCH)

            @block.gpsimd
            def _(pool):
                def rstd_of(b):
                    pool.wait_ge(mv_ready, QB * (b + 1))
                    wait(pool, y_ready, QB * b)
                    stand(pool)
                    pool.tensor_scalar(var[:, :], mv[:, :, 1], 1.0, LN_EPS, ALU.mult, ALU.add).then_inc(var_ready, 1)
                    pool.wait_ge(var_ready, b + 1)
                    pool.tensor_tensor(rstd[:, :], var[:, :], power[:, 0, 0:QB], ALU.pow).then_inc(rstd_ready, 1)
                    pool.wait_ge(rstd_ready, b + 1)
                    pool.tensor_tensor(nmr[:, :], mv[:, :, 0], rstd[:, :], ALU.mult).then_inc(mr_ready, 1)
                    pool.wait_ge(mr_ready, b + 1)
                    stand(pool)
                    pool.tensor_scalar(nmr[:, :], nmr[:, :], -1.0, 1.0, ALU.mult, ALU.mult).then_inc(nmr_ready, 1)

                def add_k(b, t):
                    pool.wait_ge(k_sin_done, QB * b + t + 1)
                    pool.tensor_tensor(k_cos[:, t, :], k_cos[:, t, :], by_sin[:, t, :], ALU.add).then_inc(k_added, 1)

                def norm_k(b):
                    pool.wait_ge(k_squared, GROUP * QB * (b + 1))
                    stand(pool)
                    pool.tensor_scalar(k_ms[:, :, :], k_ss[:, :, :], 1.0 / DH, RMS_EPS, ALU.mult, ALU.add).then_inc(k_ms_ready, 1)
                    pool.wait_ge(k_ms_ready, b + 1)
                    pool.tensor_tensor(k_rs[:, :, :], k_ms[:, :, :], power[:, :, :], ALU.pow).then_inc(k_rs_ready, 1)
                    pool.wait_ge(k_rs_ready, b + 1)
                    pool.wait_ge(k_added, QB * (b + 1))
                    for t in range(QB):
                        pool.tensor_tensor(by_head(k_cos[:, t, :]), by_head(k_cos[:, t, :]), k_rs[:, t, :, None].broadcast_to([P, KV, DH]), ALU.mult).then_inc(k_normed, 1)

                def add_q(n, t):
                    pool.wait_ge(q_sin_done, QB * n + t + 1)
                    pool.tensor_tensor(q_cos[:, t, :], q_cos[:, t, :], by_sin[:, t, :], ALU.add).then_inc(q_added, 1)

                def norm_q(n, parity):
                    pool.wait_ge(q_squared, GROUP * QB * (n + 1))
                    stand(pool)
                    pool.tensor_scalar(q_ms[:, :, :], q_ss[:, :, :], 1.0, DH * RMS_EPS, ALU.mult, ALU.add).then_inc(q_ms_ready, 1)
                    pool.wait_ge(q_ms_ready, n + 1)
                    wait(pool, exp_done, QB * GROUP * (n - 1))
                    pool.tensor_tensor(q_rs[:, parity, :, :], q_ms[:, :, :], power[:, :, :], ALU.pow).then_inc(q_rs_ready, 1)

                def scale_probs(b, g, h):
                    n = GROUP * (KV * b + g) + h
                    pool.wait_ge(inverse_ready, n + 1)
                    stand(pool)
                    for t in range(QB):
                        to = BLOCKS * P if t else P
                        at = prob[:, h, to - SPAN[t]:to]
                        pool.tensor_scalar(at, at, inverse[:, h, t:t + 1], 1.0, ALU.mult, ALU.mult).then_inc(prob_ready, 1)

                def batch(b, first, last):
                    for g in range(KV):
                        n = KV * b + g + 1
                        ahead = g < KV - 1 or not last
                        scale_probs(b, g, 0)
                        scale_probs(b, g, 1)
                        if g == KV - 1 and ahead:
                            add_k(b + 1, 0)
                            add_k(b + 1, 1)
                        if ahead:
                            add_q(n, 0)
                        scale_probs(b, g, 2)
                        scale_probs(b, g, 3)
                        if ahead:
                            add_q(n, 1)
                        if g == KV - 1 and ahead:
                            norm_k(b + 1)
                        if ahead:
                            norm_q(n, (g + 1) % 2)
                        if g == 0 and not last:
                            rstd_of(b + 1)

                pool.memset(power[:, :, :], -0.5).then_inc(set_up, 1)
                pool.memset(prob[:, :, P:2 * P], 0.0).then_inc(set_up, 1)
                pool.wait_ge(set_up, 2)
                rstd_of(0)
                add_k(0, 0)
                add_k(0, 1)
                add_q(0, 0)
                add_q(0, 1)
                norm_k(0)
                norm_q(0, 0)
                batches(pool, batch)


class Kept:

    def __init__(self, nc, stack):
        def sb(name, shape, dt):
            return stack.enter_context(nc.sbuf_tensor(name, shape, dt))

        self.x = sb("x", [P, SUB, D], F32)
        self.wqkv_hi = sb("wqkv_hi", [P, KC, QKV], F32R)
        self.wqkv_lo = sb("wqkv_lo", [P, KC, QKV], F32R)
        self.wo_hi = sb("wo_hi", [P, HEADS * D], F32R)
        self.wo_lo = sb("wo_lo", [P, HEADS * D], F32R)
        self.w8 = sb("w8", [P, M, 3 * D], BF16)
        self.gate_half = sb("gate_half", [P, M], F32)
        self.gate_up = sb("gate_up", [P, M], F32)
        self.down_s = sb("down_s", [P, D], F32)
        self.down_half = sb("down_half", [P, D], F32)
        self.rope = sb("rope", [P, 2, 2, 2, DH], F32)
        self.ident = sb("ident", [P, P], F32)
        self.mask = sb("mask", [P, 2 * P + WINDOW], F32)


def build(nc, dram, out):
    with ExitStack() as stack:
        keep = Kept(nc, stack)
        weights_phase(nc, stack, dram, keep)
        ffn_phase(nc, stack, keep, "f_")
        attention_phase(nc, stack, keep)
        ffn_phase(nc, stack, keep, "g_", out)


def constants():
    inv_freq = (1.0 / np.float32(10000.0) ** (np.arange(0, DH, 2, dtype=np.float32) / np.float32(DH))).astype(np.float32)
    freqs = np.arange(T, dtype=np.float32)[:, None] * inv_freq[None, :]
    cos, sin = np.cos(freqs), np.sin(freqs)
    q, k0, k1 = np.arange(P)[:, None], np.arange(P)[None, :], np.arange(-WINDOW, P)[None, :]
    seen = np.concatenate([(q >= k0) & (q - k0 <= WINDOW), (q >= k1) & (q - k1 <= WINDOW)], axis=1)
    return {
        "cos": np.concatenate([cos, cos], axis=1),
        "sin": np.concatenate([-sin, sin], axis=1),
        "mask": np.where(seen, np.float32(0), np.float32(MASKED)),
        "ident": np.eye(P, dtype=np.float32),
    }


def kernel(L0_attn_x, L0_attn_Wq, L0_attn_Wk, L0_attn_Wv, L0_attn_Wo, L0_attn_qn_w, L0_attn_kn_w,
           L0_ffn_gate_w, L0_ffn_up_w, L0_ffn_down_w, L0_ffn_gate_scale, L0_ffn_up_scale, L0_ffn_down_scale):
    import concourse.bacc as bacc
    from concourse.bass_utils import run_bass_kernel_spmd

    given = {
        "x": L0_attn_x,
        "wqkv_t": np.concatenate([L0_attn_Wq, L0_attn_Wk, L0_attn_Wv], axis=0).T,
        "wo_t": np.asarray(L0_attn_Wo).T,
        "qn": L0_attn_qn_w, "kn": L0_attn_kn_w,
        "gate_w": L0_ffn_gate_w, "up_w": L0_ffn_up_w, "down_w": L0_ffn_down_w,
        "gate_s": np.asarray(L0_ffn_gate_scale).reshape(M, P).T, "up_s": np.asarray(L0_ffn_up_scale).reshape(M, P).T, "down_s": L0_ffn_down_scale,
    }
    given.update(constants())
    nc = bacc.Bacc("TRN2", target_bir_lowering=False, num_devices=1)
    arrays, dram = {}, {}
    for name, a in given.items():
        a = np.ascontiguousarray(a)
        arrays[f"in_{name}"] = a
        dram[name] = nc.dram_tensor(f"in_{name}", a.shape, mybir.dt.from_np(a.dtype), kind="ExternalInput").ap()
    out = nc.dram_tensor("out", (BATCH, T, D), F32, kind="ExternalOutput").ap()
    build(nc, dram, out)
    return run_bass_kernel_spmd(nc, [arrays], core_ids=[0]).results[0]["out"]
```

```python
from contextlib import ExitStack

import numpy as np

import concourse.bass as bass
from concourse import mybir

ALU = mybir.AluOpType
ACT = mybir.ActivationFunctionType
F32 = mybir.dt.float32
F32R = mybir.dt.float32r
BF16 = mybir.dt.bfloat16
I32 = mybir.dt.int32

P = 128
BATCH, T, D = 16, 256, 256
HEADS, KV, DH = 16, 4, 128
GROUP = HEADS // KV
WINDOW = 64
I = 768
KC = D // P
M = I // P
SUB = BATCH * T // P
QKV = (HEADS + 2 * KV) * DH
LN_EPS = 1e-5
RMS_EPS = 1e-6
MASKED = -1e30

F8_MIN_NORMAL = 2.0 ** -6
F8_MAGIC = 1.5 * 2.0 ** 20
F8_OVER = float(np.float32(2.0 ** 119 * 512 / 464))


class Phase:

    def __init__(self, nc, stack, semaphores, prefix):
        self.nc, self.stack, self.semaphores, self.prefix = nc, stack, semaphores, prefix

    def sb(self, name, shape, dt):
        return self.stack.enter_context(self.nc.sbuf_tensor(self.prefix + name, shape, dt))

    def ps(self, name, shape=(P, 512), dt=F32):
        return self.stack.enter_context(self.nc.psum_tensor(self.prefix + name, list(shape), dt))

    def sem(self, name):
        return self.semaphores.enter_context(self.nc.semaphore(self.prefix + name))


def stand(eng):
    eng.nop(nofuse=True)


def product(pe, out, parts, start=True, stop=True):
    for n, (w, x) in enumerate(parts):
        last = pe.matmul(out, w, x, start=start and n == 0, stop=stop and n == len(parts) - 1,
                         skip_group_check=True)
    return last


def three(w_hi, w_lo, x_hi, x_lo):
    return [(w_hi, x_hi), (w_hi, x_lo), (w_lo, x_hi)]


def ffn_phase(nc, semaphores, keep, prefix, dram=None, out_dram=None):
    TILE = 512
    SUBS = TILE // P
    TILES = BATCH * T // TILE
    GU_AHEAD = 3
    SPLIT = 4
    EARLY = 4
    CH = 512
    RAW = 4
    LOW_AT = {1: [3, 3, 4, 4, 5, 5], TILES - 2: [1, 3, 3, 4, 4, 5, 5], TILES - 1: [1, 2, 2, 3, 3, 4, 4]}
    assert sum(len(steps) for steps in LOW_AT.values()) == (KC * QKV + HEADS * D) // CH
    with ExitStack() as stack:
        ph = Phase(nc, stack, semaphores, prefix)
        w8 = ph.sb("w8", [P, M, 3 * D], F32R)
        stats = ph.sb("stats", [P, SUBS, 6], F32)
        mv = ph.sb("mv", [P, SUBS, 2], F32)
        var = ph.sb("var", [P, SUBS], F32)
        rstd = ph.sb("rstd", [P, SUBS], F32)
        nmr = ph.sb("nmr", [P, SUBS], F32)
        power = ph.sb("power", [P, SUBS], F32)
        y = ph.sb("y", [P, SUBS, D], F32)
        yt_hi = ph.sb("yt_hi", [P, 2, KC, TILE], F32R)
        yt_lo = ph.sb("yt_lo", [P, 2, KC, TILE], F32R)
        th = ph.sb("th", [P, 2, TILE], F32)
        gated = ph.sb("gated", [P, 2, TILE], F32)
        h = ph.sb("h", [P, 2, TILE], F32)
        h_hi = ph.sb("h_hi", [P, SPLIT, TILE], F32R)
        h_lo = ph.sb("h_lo", [P, SPLIT, TILE], F32R)
        scaled = ph.sb("scaled", [P, 2, TILE], F32)

        if dram:
            raw = ph.sb("raw", [P, RAW, CH], F32)
            raw_loaded = [ph.sem(f"raw_loaded{k}") for k in range(RAW)]
            raw8, magic, q8, over, raw_scale, down_s, wrow, rope_raw = keep.early
            x_loaded = [ph.sem(f"x_loaded{t}") for t in range(TILES)]
            ffn_loaded = [ph.sem(f"ffn_loaded{m}") for m in range(M)]
            scales_loaded = ph.sem("scales_loaded")
            down_s_loaded = ph.sem("down_s_loaded")
            ident_loaded = ph.sem("ident_loaded")
            rope_loaded = ph.sem("rope_loaded")
            mask_loaded = ph.sem("mask_loaded")
            exponent = ph.sem("exponent")
            magic_ready = ph.sem("magic_ready")
            added = ph.sem("added")
            rounded = ph.sem("rounded")
            scaled_over = ph.sem("scaled_over")
            over_ready = ph.sem("over_ready")
            w8_kept = ph.sem("w8_kept")
            scales_ready = ph.sem("scales_ready")
            one_plus = ph.sem("one_plus")
            rope_ready = ph.sem("rope_ready")
            raw_hi = ph.sem("raw_hi")
            raw_split = ph.sem("raw_split")

        def chunks():
            wqkv = dram["wqkv_t"].rearrange("(k p) n -> p k n", p=P)
            wo = dram["wo_t"].rearrange("(h p) n -> p h n", p=P)
            found = []
            for k in range(KC):
                for c in range(QKV // CH):
                    at = slice(c * CH, (c + 1) * CH)
                    found.append((wqkv[:, k, at], keep.wqkv_hi[:, k, at], keep.wqkv_lo[:, k, at]))
            for c in range(HEADS * D // CH):
                at = slice(c * CH, (c + 1) * CH)
                heads = slice(c * CH // D, (c + 1) * CH // D)
                found.append((wo[:, heads, :], keep.wo_hi[:, at], keep.wo_lo[:, at]))
            return found

        gate = [ph.ps(f"gate{k}") for k in range(2)]
        up = [ph.ps(f"up{k}") for k in range(2)]
        turn = [ph.ps(f"turn{k}") for k in range(KC)]
        acc = [ph.ps(f"acc{k}") for k in range(2)]

        w8_ready = ph.sem("w8_ready")
        stats_done = ph.sem("stats_done")
        mv_ready = ph.sem("mv_ready")
        power_set = ph.sem("power_set")
        var_ready = ph.sem("var_ready")
        rstd_ready = ph.sem("rstd_ready")
        mr_ready = ph.sem("mr_ready")
        nmr_ready = ph.sem("nmr_ready")
        y_ready = ph.sem("y_ready")
        turned = ph.sem("turned")
        yt_hi_ready = ph.sem("yt_hi_ready")
        yt_ready = ph.sem("yt_ready")
        gate_ready = ph.sem("gate_ready")
        up_ready = ph.sem("up_ready")
        th_ready = ph.sem("th_ready")
        gate_used = ph.sem("gate_used")
        h_ready = ph.sem("h_ready")
        h_hi_ready = ph.sem("h_hi_ready")
        h_split = ph.sem("h_split")
        down_done = ph.sem("down_done")
        acc_used = ph.sem("acc_used")
        x_done = ph.sem("x_done")
        stored = ph.sem("stored")

        def wait(eng, sem, value):
            if not isinstance(value, int) or value > 0:
                eng.wait_ge(sem, value)

        def h_place(t, parity, m):
            return (parity * M + m) % SPLIT

        def norm_late(t):
            return bool(dram) and isinstance(t, int) and t == 0

        def chunks_of_step(t, m):
            if not dram or not isinstance(t, int):
                return []
            before = sum(len(steps) for tile, steps in LOW_AT.items() if tile < t)
            return [before + n for n, at in enumerate(LOW_AT.get(t, [])) if at == m]

        def pairs(eng, tile):
            tile(0, 0, 0, 2)
            tile(1, 1, 1, 2)
            with eng.Fori(1, TILES // 2 - 1) as pair:
                tile(2 * pair, 0, 2, 2)
                tile(2 * pair + 1, 1, 2, 2)
            tile(TILES - 2, 0, 2, 1)
            tile(TILES - 1, 1, 2, 0)

        def x_of(t):
            return keep.x[:, bass.ds(t * SUBS, SUBS), :]

        def load_x(eng, t):
            x_in = dram["x"].rearrange("b (t p) d -> p (b t) d", p=P)
            eng.dma_start(x_of(t), x_in[:, t * SUBS:(t + 1) * SUBS, :]).then_inc(x_loaded[t], 16)

        with nc.Block() as block:

            @block.tensor
            def _(pe):
                def turn_y(t):
                    pe.wait_ge(y_ready, SUBS * (t + 1))
                    wait(pe, yt_ready, KC * t)
                    for k in range(KC):
                        for s in range(SUBS):
                            last = pe.transpose(turn[k][:, s * P:(s + 1) * P], y[:, s, k * P:(k + 1) * P], keep.ident[:, :])
                        last.then_inc(turned, 1)

                def gate_up(t, parity, m):
                    step = t * M + m
                    if isinstance(t, int) and t == 0:
                        pe.wait_ge(w8_ready, m + 1 if dram else 2)
                    if m == 0:
                        pe.wait_ge(yt_ready, KC * (t + 1))
                    wait(pe, gate_used, step - 1)
                    for a, (bank, ready) in enumerate(((gate[m % 2], gate_ready), (up[m % 2], up_ready))):
                        if a:
                            wait(pe, h_ready, step - 1)
                        parts = []
                        for k in range(KC):
                            w = w8[:, m, a * D + k * P:a * D + (k + 1) * P]
                            parts += [(w, yt_hi[:, parity, k, :]), (w, yt_lo[:, parity, k, :])]
                        product(pe, bank[:, :], parts).then_inc(ready, 1)

                def down(t, parity, m):
                    step = t * M + m
                    pe.wait_ge(h_split, step + 1)
                    place = h_place(t, parity, m)
                    if m == 0:
                        wait(pe, acc_used, 2 * t)
                    w = w8[:, m, 2 * D:]
                    for s in range(SUBS):
                        at = slice(s * P, (s + 1) * P)
                        out = acc[s // 2][:, (s % 2) * D:(s % 2 + 1) * D]
                        last = product(pe, out, [(h_hi[:, place, at], w), (h_lo[:, place, at], w)],
                                       start=(m == 0 and s % 2 == 0), stop=(m == M - 1))
                    last.then_inc(down_done, 1)

                def tile(t, parity, before, after):
                    for m in range(M):
                        if m + GU_AHEAD < M:
                            gate_up(t, parity, m + GU_AHEAD)
                        elif after:
                            gate_up(t + 1, 1 - parity, m + GU_AHEAD - M)
                        down(t, parity, m)
                        if m == 0 and after:
                            turn_y(t + 1)

                if dram:
                    pe.wait_ge(ident_loaded, 16)
                turn_y(0)
                for m in range(GU_AHEAD):
                    gate_up(0, 0, m)
                pairs(pe, tile)

            @block.scalar
            def _(act):
                def normalise(t, subs):
                    act.wait_ge(nmr_ready, t + 1)
                    wait(act, turned, KC * t)
                    for s in subs:
                        act.activation(y[:, s, :], keep.x[:, bass.ds(t * SUBS + s, 1), :].rearrange("p a d -> p (a d)"), ACT.Identity,
                                       bias=nmr[:, s:s + 1], scale=rstd[:, s:s + 1]).then_inc(y_ready, 1)

                def yt_high(t, parity):
                    for k in range(KC):
                        act.wait_ge(turned, KC * t + k + 1)
                        if k == 0:
                            wait(act, up_ready, M * (t - 1))
                        act.activation(yt_hi[:, parity, k, :], turn[k][:, :], ACT.Copy).then_inc(yt_hi_ready, 1)

                def tanh(t, m):
                    step = t * M + m
                    act.wait_ge(gate_ready, step + 1)
                    wait(act, gate_used, step - 1)
                    act.activation(th[:, m % 2, :], gate[m % 2][:, :], ACT.Tanh, scale=keep.gate_half[:, m:m + 1]).then_inc(th_ready, 1)

                def tile(t, parity, before, after):
                    for m in range(M):
                        step = t * M + m
                        if m + 1 < M:
                            tanh(t, m + 1)
                        elif after:
                            tanh(t + 1, 0)
                        act.wait_ge(h_ready, step + 1)
                        wait(act, down_done, step - SPLIT + 1)
                        act.activation(h_hi[:, h_place(t, parity, m), :], h[:, m % 2, :], ACT.Copy).then_inc(h_hi_ready, 1)
                        first = dram and isinstance(t, int) and t == 0
                        if first and m >= M // 2:
                            for k in (2 * m - M, 2 * m - M + 1):
                                act.wait_ge(w8_ready, k + 1)
                                act.activation(keep.w8[:, k, :], w8[:, k, :].bitcast(F32), ACT.Copy).then_inc(w8_kept, 1)
                        for n in chunks_of_step(t, m + 1):
                            if n == 0:
                                act.wait_ge(w8_ready, M)
                                act.wait_ge(scales_ready, 3)
                                act.wait_ge(rope_ready, 8)
                            act.wait_ge(raw_loaded[n % RAW], 16 * (n // RAW + 1))
                            act.activation(chunks()[n][1], raw[:, n % RAW, :], ACT.Copy).then_inc(raw_hi, 1)
                        if m == 2 and after:
                            yt_high(t + 1, 1 - parity)
                        if first and m + EARLY < M:
                            overflow(m + EARLY)
                        if m == 5 and after == 2 and norm_late(t):
                            normalise(t + 2, range(SUBS))
                        elif m in (4, 5) and after == 2 and not norm_late(t):
                            normalise(t + 2, range(2 * (m - 4), 2 * (m - 3)))

                def overflow(m):
                    act.wait_ge(rounded, m + 1)
                    wait(act, w8_ready, m - 1)
                    act.activation(over[:, m % 2, :], q8[:, m % 2, :], ACT.Copy, scale=F8_OVER).then_inc(scaled_over, 1)
                    act.wait_ge(scaled_over, m + 1)
                    act.activation(over[:, m % 2, :], over[:, m % 2, :], ACT.Copy, scale=0.0).then_inc(over_ready, 1)

                if dram:
                    load_x(act, 0)
                    act.dma_start(keep.ident[:, :], dram["ident"]).then_inc(ident_loaded, 16)
                    act.dma_start(raw_scale[:, 0, :], dram["gate_s"]).then_inc(scales_loaded, 16)
                    act.dma_start(raw_scale[:, 1, :], dram["up_s"]).then_inc(scales_loaded, 16)
                    load_x(act, 1)
                    normalise(0, range(SUBS))
                    overflow(0)
                    yt_high(0, 0)
                    for m in range(1, EARLY):
                        overflow(m)
                else:
                    act.activation(w8[:, 0:M // 2, :], keep.w8[:, 0:M // 2, :], ACT.Copy).then_inc(w8_ready, 1)
                    normalise(0, range(SUBS))
                    yt_high(0, 0)
                if dram:
                    act.wait_ge(scales_ready, 2)
                tanh(0, 0)
                normalise(1, range(SUBS))
                pairs(act, tile)

            @block.vector
            def _(dve):
                def statistics(t):
                    wait(dve, nmr_ready, t)
                    if dram and isinstance(t, int) and t < 4:
                        for part in range(t, t + 1 if t < 3 else TILES):
                            dve.wait_ge(x_loaded[part], 16)
                    for s in range(SUBS):
                        dve.bn_stats(stats[:, s, :], keep.x[:, bass.ds(t * SUBS + s, 1), :].rearrange("p a d -> p (a d)")).then_inc(stats_done, 1)
                    for s in range(SUBS):
                        dve.wait_ge(stats_done, SUBS * t + s + 1)
                        stand(dve)
                        dve.bn_aggr(mv[:, s, :], stats[:, s, :]).then_inc(mv_ready, 1)

                def yt_low(t, parity):
                    for k in range(KC):
                        dve.wait_ge(yt_hi_ready, KC * t + k + 1)
                        dve.tensor_tensor(yt_lo[:, parity, k, :], turn[k][:, :], yt_hi[:, parity, k, :].bitcast(F32), ALU.subtract).then_inc(yt_ready, 1)

                def scale_sums(t):
                    dve.wait_ge(down_done, M * (t + 1))
                    if dram and isinstance(t, int) and t == 0:
                        dve.wait_ge(scales_ready, 3)
                    wait(dve, x_done, 2 * t)
                    for k in range(2):
                        scale = keep.down_half[:, None, :].broadcast_to([P, 2, D])
                        dve.tensor_tensor(scaled[:, k, :].rearrange("p (s d) -> p s d", d=D), acc[k][:, :].rearrange("p (s d) -> p s d", d=D),
                                          scale, ALU.mult).then_inc(acc_used, 1)

                def tile(t, parity, before, after):
                    for m in range(M):
                        step = t * M + m
                        dve.wait_ge(th_ready, step + 1)
                        dve.scalar_tensor_tensor(gated[:, m % 2, :], th[:, m % 2, :], 1.0, gate[m % 2][:, :], ALU.add, ALU.mult).then_inc(gate_used, 1)
                        dve.wait_ge(up_ready, step + 1)
                        dve.wait_ge(gate_used, step + 1)
                        wait(dve, h_split, step - 1)
                        dve.scalar_tensor_tensor(h[:, m % 2, :], up[m % 2][:, :], keep.gate_up[:, m:m + 1], gated[:, m % 2, :], ALU.mult, ALU.mult).then_inc(h_ready, 1)
                        if m == 1 and before:
                            scale_sums(t - 1)
                        if m == 2 and after:
                            yt_low(t + 1, 1 - parity)
                        if m == (4 if norm_late(t) else 0) and after == 2:
                            statistics(t + 2)
                        first = dram and isinstance(t, int) and t == 0
                        if first and m + EARLY < M:
                            round_weights(m + EARLY)
                        if dram and isinstance(t, int) and t == 1 and m == 0:
                            rope_tables()
                        for n in chunks_of_step(t, m):
                            hi, lo = chunks()[n][1:]
                            dve.wait_ge(raw_hi, n + 1)
                            dve.tensor_tensor(lo, raw[:, n % RAW, :], hi.bitcast(F32), ALU.subtract).then_inc(raw_split, 1)

                def round_weights(m):
                    w, mg, q = raw8[:, m, :], magic[:, m % 2, :], q8[:, m % 2, :]
                    dve.wait_ge(ffn_loaded[m], 16 * 3)
                    wait(dve, rounded, m - 1)
                    dve.tensor_scalar(mg.bitcast(I32), w.bitcast(I32), 0x7F800000, None, ALU.bitwise_and).then_inc(exponent, 1)
                    dve.wait_ge(exponent, m + 1)
                    dve.tensor_scalar(mg, mg, F8_MIN_NORMAL, F8_MAGIC, ALU.max, ALU.mult).then_inc(magic_ready, 1)
                    dve.wait_ge(magic_ready, m + 1)
                    dve.tensor_tensor(w, w, mg, ALU.add).then_inc(added, 1)
                    dve.wait_ge(added, m + 1)
                    wait(dve, w8_ready, m - 1)
                    dve.tensor_tensor(q, w, mg, ALU.subtract).then_inc(rounded, 1)

                def scale_tables():
                    dve.wait_ge(scales_loaded, 16 * 2)
                    dve.tensor_scalar(keep.gate_half[:, :], raw_scale[:, 0, :], 0.5, None, ALU.mult).then_inc(scales_ready, 1)
                    dve.scalar_tensor_tensor(keep.gate_up[:, :], raw_scale[:, 0, :], 0.5, raw_scale[:, 1, :], ALU.mult, ALU.mult).then_inc(scales_ready, 1)

                def rope_tables():
                    dve.wait_ge(down_s_loaded, 16)
                    dve.tensor_scalar(keep.down_half[:, :], down_s[:, :], 0.5, None, ALU.mult).then_inc(scales_ready, 1)
                    dve.wait_ge(rope_loaded, 16 * 4)
                    dve.tensor_scalar(wrow[:, :, :], wrow[:, :, :], 1.0, None, ALU.add).then_inc(one_plus, 1)
                    dve.wait_ge(one_plus, 1)
                    for n in range(2):
                        w = wrow[:, n, :]
                        swapped = w.rearrange("p (s d) -> p s d", s=2)[:, ::-1, :]
                        for t in range(2):
                            dve.tensor_tensor(keep.rope[:, n, 0, t, :], rope_raw[:, 0, t, :], w, ALU.mult).then_inc(rope_ready, 1)
                            dve.tensor_tensor(keep.rope[:, n, 1, t, :].rearrange("p (s d) -> p s d", s=2),
                                              rope_raw[:, 1, t, :].rearrange("p (s d) -> p s d", s=2), swapped, ALU.mult).then_inc(rope_ready, 1)

                if dram:
                    statistics(0)
                    round_weights(0)
                    scale_tables()
                    round_weights(1)
                    yt_low(0, 0)
                    for m in range(2, EARLY):
                        round_weights(m)
                    statistics(1)
                    dve.wait_ge(scales_ready, 2)
                else:
                    dve.tensor_copy(w8[:, M // 2:, :], keep.w8[:, M // 2:, :]).then_inc(w8_ready, 1)
                    statistics(0)
                    statistics(1)
                    yt_low(0, 0)
                pairs(dve, tile)
                scale_sums(TILES - 1)

            @block.gpsimd
            def _(pool):
                def rstd_of(t):
                    pool.wait_ge(mv_ready, SUBS * (t + 1))
                    wait(pool, y_ready, SUBS * t)
                    stand(pool)
                    pool.tensor_scalar(var[:, :], mv[:, :, 1], 1.0, LN_EPS, ALU.mult, ALU.add).then_inc(var_ready, 1)
                    pool.wait_ge(var_ready, t + 1)
                    pool.tensor_tensor(rstd[:, :], var[:, :], power[:, :], ALU.pow).then_inc(rstd_ready, 1)
                    pool.wait_ge(rstd_ready, t + 1)
                    pool.tensor_tensor(nmr[:, :], mv[:, :, 0], rstd[:, :], ALU.mult).then_inc(mr_ready, 1)
                    pool.wait_ge(mr_ready, t + 1)
                    stand(pool)
                    pool.tensor_scalar(nmr[:, :], nmr[:, :], -1.0, 1.0, ALU.mult, ALU.mult).then_inc(nmr_ready, 1)

                def finish_weights(m):
                    pool.wait_ge(over_ready, m + 1)
                    pool.tensor_tensor(w8[:, m, :], q8[:, m % 2, :], over[:, m % 2, :], ALU.add).then_inc(w8_ready, 1)

                def add_to_x(t, k):
                    pool.wait_ge(acc_used, 2 * t + k + 1)
                    at = keep.x[:, bass.ds(t * SUBS + 2 * k, 2), :].rearrange("p s d -> p (s d)")
                    pool.tensor_tensor(at, at, scaled[:, k, :], ALU.add).then_inc(x_done, 1)

                def tile(t, parity, before, after):
                    for m in range(M):
                        step = t * M + m
                        pool.wait_ge(h_hi_ready, step + 1)
                        place = h_place(t, parity, m)
                        pool.tensor_tensor(h_lo[:, place, :], h[:, m % 2, :], h_hi[:, place, :].bitcast(F32), ALU.subtract).then_inc(h_split, 1)
                        if dram and isinstance(t, int) and t == 0 and m + EARLY < M:
                            finish_weights(m + EARLY)
                        if m in (1, 2) and before:
                            add_to_x(t - 1, m - 1)
                        if m == (4 if norm_late(t) else 3) and after == 2:
                            rstd_of(t + 2)

                pool.memset(power[:, :], -0.5).then_inc(power_set, 1)
                pool.wait_ge(power_set, 1)
                rstd_of(0)
                if dram:
                    for m in range(EARLY):
                        finish_weights(m)
                rstd_of(1)
                pairs(pool, tile)
                add_to_x(TILES - 1, 0)
                add_to_x(TILES - 1, 1)

            @block.sync
            def _(sp):
                if dram:
                    gate_w = dram["gate_w"].rearrange("(k p) (m i) -> m p k i", p=P, i=P)
                    up_w = dram["up_w"].rearrange("(k p) (m i) -> m p k i", p=P, i=P)
                    down_w = dram["down_w"].rearrange("(m p) d -> m p d", p=P)
                    for m in range(M):
                        three_w = raw8[:, m, :].rearrange("p (a k i) -> p a k i", a=3, k=KC)
                        sp.dma_start(three_w[:, 0], gate_w[m]).then_inc(ffn_loaded[m], 16)
                        sp.dma_start(three_w[:, 1], up_w[m]).then_inc(ffn_loaded[m], 16)
                        sp.dma_start(raw8[:, m, 2 * D:], down_w[m]).then_inc(ffn_loaded[m], 16)
                        if m == GU_AHEAD:
                            sp.dma_start(down_s[:, :], dram["down_s"].partition_broadcast(P)).then_inc(down_s_loaded, 16)
                            load_x(sp, 2)
                    for t in range(3, TILES):
                        load_x(sp, t)
                    sp.dma_start(wrow[:, 0, :], dram["qn"].partition_broadcast(P)).then_inc(rope_loaded, 16)
                    sp.dma_start(wrow[:, 1, :], dram["kn"].partition_broadcast(P)).then_inc(rope_loaded, 16)
                    sp.dma_start(rope_raw[:, 0], dram["cos"].rearrange("(t p) d -> p t d", p=P)).then_inc(rope_loaded, 16)
                    sp.dma_start(rope_raw[:, 1], dram["sin"].rearrange("(t p) d -> p t d", p=P)).then_inc(rope_loaded, 16)
                    sp.dma_start(keep.mask[:, :], dram["mask"]).then_inc(mask_loaded, 16)
                    for n, (src, _hi, _lo) in enumerate(chunks()):
                        if n >= RAW:
                            sp.wait_ge(raw_split, n - RAW + 1)
                        place = raw[:, n % RAW, :]
                        if n >= KC * QKV // CH:
                            place = place.rearrange("p (h n) -> p h n", n=D)
                        sp.dma_start(place, src).then_inc(raw_loaded[n % RAW], 16)
                    sp.wait_ge(mask_loaded, 16)
                if out_dram is not None:
                    view = out_dram.rearrange("b (t p) d -> p (b t) d", p=P)
                    with sp.Fori(0, TILES) as t:
                        sp.wait_ge(x_done, 2 * t + 2)
                        sp.dma_start(view[:, bass.ds(t * SUBS, SUBS), :], x_of(t)).then_inc(stored, 16)
                    sp.wait_ge(stored, 16 * TILES)


RING = 7


def stages(b, g):
    if not isinstance(b, int):
        return True, True, True, True
    n, end = KV * b + g, KV * BATCH
    return n < end, n + 1 < end, 1 <= n <= end, n >= 2


def fills_of_batch(b):
    fills = []
    for g in range(KV if b < BATCH else 2):
        here, ahead, turns, sums = stages(b, g)
        two = [0, 1]
        order = [("J", [0], ahead), ("C", two, sums), ("P", [0, 1], turns), ("J", [1], ahead), ("P", [2, 3], turns),
                 ("Y", [0], ahead and g == KV - 2 and b < BATCH - 1), ("S", range(GROUP), here),
                 ("V", two, here and g == 1), ("K", two, here and g == KV - 2 and b < BATCH - 1),
                 ("Q", two, ahead), ("T", two, ahead and g == KV - 1)]
        fills += [(what, g, part) for what, parts, used in order if used for part in parts]
    return fills


BEFORE = [("Y", KV - 2, 0), ("K", KV - 2, 0), ("K", KV - 2, 1)] + [(what, KV - 1, t) for what in "JTQ" for t in range(2)]
FIRST, STEADY, LAST, AFTER = (fills_of_batch(b) for b in (0, 1, BATCH - 1, BATCH))
assert len(STEADY) % RING == 0 and FIRST[-RING:] == STEADY[-RING:]


class Fills:

    def __init__(self, b):
        self.b = b
        at = b if isinstance(b, int) else 1
        steady = len(BEFORE) + len(FIRST)
        self.own = {-1: BEFORE, 0: FIRST, BATCH - 1: LAST, BATCH: AFTER}.get(at, STEADY)
        self.former = {-1: [], 0: BEFORE, BATCH: LAST}.get(at, STEADY)
        self.start = {-1: 0, 0: len(BEFORE), BATCH: steady + len(LAST)}.get(at, steady)

    def bank(self, what, g, part):
        return (self.start + self.own.index((what, g, part))) % RING

    def contents_before(self, what, g, part):
        n = self.own.index((what, g, part)) - RING
        if n >= 0:
            return self.own[n], self.b
        return (self.former[n], self.b - 1) if self.former else None


def attention_phase(nc, semaphores, keep):
    QB = T // P
    SPAN = [P, P + WINDOW]
    SPANS = sum(SPAN)
    BLOCKS = 3
    HW = GROUP * P
    K_AT, V_AT = HEADS * DH, (HEADS + KV) * DH
    with ExitStack() as stack:
        ph = Phase(nc, stack, semaphores, "a_")
        stats = ph.sb("stats", [P, QB, 6], F32)
        mv = ph.sb("mv", [P, QB, 2], F32)
        var = ph.sb("var", [P, QB], F32)
        rstd = ph.sb("rstd", [P, QB], F32)
        nmr = ph.sb("nmr", [P, QB], F32)
        power = ph.sb("power", [P, QB, GROUP], F32)
        y = ph.sb("y", [P, QB, D], F32)
        yt_hi = ph.sb("yt_hi", [P, KC, T], F32R)
        yt_lo = ph.sb("yt_lo", [P, KC, T], F32R)
        q_cos = ph.sb("q_cos", [P, QB, HW], F32)
        k_cos = ph.sb("k_cos", [P, QB, HW], F32)
        q_sin = ph.sb("q_sin", [P, QB, HW], F32)
        k_sin = ph.sb("k_sin", [P, QB, HW], F32)
        squares = ph.sb("squares", [P, QB, HW], BF16)
        q_ss = ph.sb("q_ss", [P, QB, GROUP], F32)
        k_ss = ph.sb("k_ss", [P, QB, KV], F32)
        q_ms = ph.sb("q_ms", [P, QB, GROUP], F32)
        k_ms = ph.sb("k_ms", [P, QB, KV], F32)
        q_rs = ph.sb("q_rs", [P, 2, QB, GROUP], F32)
        k_rs = ph.sb("k_rs", [P, QB, KV], F32)
        qt_hi = ph.sb("qt_hi", [P, QB, HW], F32R)
        qt_lo = ph.sb("qt_lo", [P, QB, HW], F32R)
        kt_hi = ph.sb("kt_hi", [P, KV, T], F32R)
        kt_lo = ph.sb("kt_lo", [P, KV, T], F32R)
        v_hi = ph.sb("v_hi", [P, QB, HW], F32R)
        v_lo = ph.sb("v_lo", [P, QB, HW], F32R)
        masked = ph.sb("masked", [P, GROUP, SPANS], F32)
        top = ph.sb("top", [P, GROUP, QB], F32)
        minus_top = ph.sb("minus_top", [P, GROUP, QB], F32)
        prob = ph.sb("prob", [P, GROUP, BLOCKS * P], F32)
        total = ph.sb("total", [P, GROUP, QB], F32)
        inverse = ph.sb("inverse", [P, GROUP, QB], F32)
        pt_hi = ph.sb("pt_hi", [P, BLOCKS, HW], F32R)
        pt_lo = ph.sb("pt_lo", [P, BLOCKS, HW], F32R)
        ctx_hi = ph.sb("ctx_hi", [P, QB, HW], F32R)
        ctx_lo = ph.sb("ctx_lo", [P, QB, HW], F32R)

        ring = [ph.ps(f"ring{k}") for k in range(RING)]
        out = ph.ps("out")

        stats_done = ph.sem("stats_done")
        mv_ready = ph.sem("mv_ready")
        set_up = ph.sem("set_up")
        var_ready = ph.sem("var_ready")
        rstd_ready = ph.sem("rstd_ready")
        mr_ready = ph.sem("mr_ready")
        nmr_ready = ph.sem("nmr_ready")
        y_ready = ph.sem("y_ready")
        y_turned = ph.sem("y_turned")
        yt_hi_ready = ph.sem("yt_hi_ready")
        yt_ready = ph.sem("yt_ready")
        k_projected = ph.sem("k_projected")
        k_cos_done = ph.sem("k_cos_done")
        k_sin_done = ph.sem("k_sin_done")
        k_squared = ph.sem("k_squared")
        k_added = ph.sem("k_added")
        k_ms_ready = ph.sem("k_ms_ready")
        k_rs_ready = ph.sem("k_rs_ready")
        k_normed = ph.sem("k_normed")
        k_turned = ph.sem("k_turned")
        kt_hi_ready = ph.sem("kt_hi_ready")
        kt_ready = ph.sem("kt_ready")
        v_projected = ph.sem("v_projected")
        v_hi_ready = ph.sem("v_hi_ready")
        v_ready = ph.sem("v_ready")
        q_projected = ph.sem("q_projected")
        q_cos_done = ph.sem("q_cos_done")
        q_sin_done = ph.sem("q_sin_done")
        q_squared = ph.sem("q_squared")
        q_added = ph.sem("q_added")
        q_ms_ready = ph.sem("q_ms_ready")
        q_rs_ready = ph.sem("q_rs_ready")
        q_turned = ph.sem("q_turned")
        qt_hi_ready = ph.sem("qt_hi_ready")
        qt_ready = ph.sem("qt_ready")
        scored = ph.sem("scored")
        top_ready = ph.sem("top_ready")
        bias_ready = ph.sem("bias_ready")
        exp_done = ph.sem("exp_done")
        inverse_ready = ph.sem("inverse_ready")
        prob_ready = ph.sem("prob_ready")
        p_turned = ph.sem("p_turned")
        pt_hi_ready = ph.sem("pt_hi_ready")
        pt_ready = ph.sem("pt_ready")
        ctx_summed = ph.sem("ctx_summed")
        ctx_hi_ready = ph.sem("ctx_hi_ready")
        ctx_ready = ph.sem("ctx_ready")
        projected = ph.sem("projected")
        out_used = ph.sem("out_used")

        def wait(eng, sem, value):
            if not isinstance(value, int) or value > 0:
                eng.wait_ge(sem, value)

        def batches(eng, slot):
            def batch(b):
                for g in range(KV):
                    slot(b, g)

            batch(0)
            with eng.Fori(1, BATCH - 1) as b:
                batch(b)
            batch(BATCH - 1)
            slot(BATCH, 0)
            slot(BATCH, 1)

        def x_sub(b, t):
            return keep.x[:, bass.ds(b * QB + t, 1), :].rearrange("p a d -> p (a d)")

        def by_head(ap):
            return ap.rearrange("p (h d) -> p h d", h=GROUP)

        def halves(ap):
            return ap.rearrange("p (h s d) -> p h s d", h=GROUP, s=2)

        with nc.Block() as block:

            @block.tensor
            def _(pe):
                readers = {
                    "S": lambda b, g, h: (top_ready, QB * (GROUP * (KV * b + g) + h + 1)),
                    "J": lambda b, g, t: (q_squared, GROUP * (QB * (KV * b + g + 1) + t + 1)),
                    "K": lambda b, g, t: (k_squared, GROUP * (QB * (b + 1) + t + 1)),
                    "V": lambda b, g, t: (v_ready, QB * b + t + 1),
                    "C": lambda b, g, t: (ctx_ready, QB * (KV * b + g - 2) + t + 1),
                    "P": lambda b, g, h: (pt_ready, GROUP * (KV * b + g - 1) + h + 1),
                    "Y": lambda b, g, _: (yt_ready, b + 2),
                    "T": lambda b, g, t: (kt_ready, QB * (b + 1) + t + 1),
                    "Q": lambda b, g, t: (qt_ready, QB * (KV * b + g + 1) + t + 1),
                }

                def begin(f, what, g, part):
                    before = f.contents_before(what, g, part)
                    if before:
                        (what0, g0, part0), b0 = before
                        pe.wait_ge(*readers[what0](b0, g0, part0))
                    return ring[f.bank(what, g, part)]

                def turn_y(f):
                    b = f.b + 1
                    bank = begin(f, "Y", KV - 2, 0)
                    pe.wait_ge(y_ready, QB * (b + 1))
                    for k in range(KC):
                        for t in range(QB):
                            last = pe.transpose(bank[:, k * T + t * P:k * T + (t + 1) * P], y[:, t, k * P:(k + 1) * P], keep.ident[:, :])
                    last.then_inc(y_turned, 1)

                def project(f, what, g, b, at, done, subs=range(QB)):
                    for t in subs:
                        bank = begin(f, what, g, t)
                        pe.wait_ge(yt_ready, b + 1)
                        parts = []
                        for k in range(KC):
                            tok = slice(t * P, (t + 1) * P)
                            parts += three(yt_hi[:, k, tok], yt_lo[:, k, tok], keep.wqkv_hi[:, k, at:at + HW], keep.wqkv_lo[:, k, at:at + HW])
                        product(pe, bank[:, :], parts).then_inc(done, 1)

                def turn_heads(bank, src, done):
                    for h in range(GROUP):
                        at = slice(h * P, (h + 1) * P)
                        last = pe.transpose(bank[:, at], src[:, at], keep.ident[:, :])
                    last.then_inc(done, 1)

                def turn_q(f, g, subs=range(QB)):
                    for t in subs:
                        bank = begin(f, "Q", g, t)
                        pe.wait_ge(q_added, QB * (KV * f.b + g + 1) + t + 1)
                        turn_heads(bank, q_cos[:, t, :], q_turned)

                def turn_k(f):
                    for t in range(QB):
                        bank = begin(f, "T", KV - 1, t)
                        pe.wait_ge(k_normed, QB * (f.b + 1) + t + 1)
                        turn_heads(bank, k_cos[:, t, :], k_turned)

                def scores(f, g, h):
                    bank = begin(f, "S", g, h)
                    if h == 0:
                        pe.wait_ge(qt_ready, QB * (KV * f.b + g + 1))
                        pe.wait_ge(kt_ready, QB * (f.b + 1))
                    at = slice(h * P, (h + 1) * P)
                    first = 0
                    for t in range(QB):
                        keys = slice((t + 1) * P - SPAN[t], (t + 1) * P)
                        last = product(pe, bank[:, first:first + SPAN[t]],
                                       three(qt_hi[:, t, at], qt_lo[:, t, at], kt_hi[:, g, keys], kt_lo[:, g, keys]))
                        first += SPAN[t]
                    last.then_inc(scored, 1)

                def turn_probs(f, g, h):
                    bank = begin(f, "P", g, h)
                    pe.wait_ge(prob_ready, QB * (GROUP * (KV * f.b + g - 1) + h + 1))
                    for k in range(BLOCKS):
                        last = pe.transpose(bank[:, k * P:(k + 1) * P], prob[:, h, k * P:(k + 1) * P], keep.ident[:, :])
                    last.then_inc(p_turned, 1)

                def context(f, g):
                    n = KV * f.b + g - 2
                    v_at = slice((g - 2) % KV * DH, ((g - 2) % KV + 1) * DH)
                    pe.wait_ge(pt_ready, GROUP * (n + 1))
                    pe.wait_ge(v_ready, QB * (f.b + 1) if g >= 2 else QB * f.b)
                    for t in range(QB):
                        bank = begin(f, "C", g, t)
                        parts = []
                        for k in range(t + 1):
                            parts += three(v_hi[:, k, v_at], v_lo[:, k, v_at], pt_hi[:, t + k, :], pt_lo[:, t + k, :])
                        product(pe, bank[:, :], parts).then_inc(ctx_summed, 1)

                def out_projection(b, g, t):
                    n = KV * b + g - 2
                    g = (g - 2) % KV
                    pe.wait_ge(ctx_ready, QB * n + t + 1)
                    if g == 0 and t == 0:
                        wait(pe, out_used, b)
                    for h in range(GROUP):
                        at = slice(h * P, (h + 1) * P)
                        w = slice((g * GROUP + h) * D, (g * GROUP + h + 1) * D)
                        last = product(pe, out[:, t * D:(t + 1) * D],
                                       three(ctx_hi[:, t, at], ctx_lo[:, t, at], keep.wo_hi[:, w], keep.wo_lo[:, w]),
                                       start=(g == 0 and t == 0 and h == 0), stop=(g == KV - 1 and h == GROUP - 1))
                    last.then_inc(projected, 1)

                def slot(b, g):
                    f = Fills(b)
                    here, ahead, turns, sums = stages(b, g)
                    next_q = (b, (g + 1) * HW) if g < KV - 1 else (b + 1, 0)
                    if ahead:
                        project(f, "J", g, *next_q, q_projected, [0])
                    if sums:
                        context(f, g)
                    if turns:
                        turn_probs(f, g, 0)
                        turn_probs(f, g, 1)
                    if ahead:
                        project(f, "J", g, *next_q, q_projected, [1])
                    if turns:
                        turn_probs(f, g, 2)
                        turn_probs(f, g, 3)
                    if ("Y", g, 0) in f.own:
                        turn_y(f)
                    if here:
                        scores(f, g, 0)
                        scores(f, g, 1)
                    if sums:
                        out_projection(b, g, 0)
                    if here:
                        scores(f, g, 2)
                        scores(f, g, 3)
                    if ("V", g, 0) in f.own:
                        project(f, "V", g, b, V_AT, v_projected)
                    if ("K", g, 0) in f.own:
                        project(f, "K", g, b + 1, K_AT, k_projected)
                    if ahead:
                        turn_q(f, g, [0])
                    if sums:
                        out_projection(b, g, 1)
                    if ahead:
                        turn_q(f, g, [1])
                    if ("T", g, 0) in f.own:
                        turn_k(f)

                f = Fills(-1)
                pe.wait_ge(set_up, 2)
                turn_y(f)
                project(f, "K", KV - 2, 0, K_AT, k_projected)
                project(f, "J", KV - 1, 0, 0, q_projected)
                turn_k(f)
                turn_q(f, KV - 1)
                batches(pe, slot)

            @block.scalar
            def _(act):
                def normalise(b):
                    act.wait_ge(nmr_ready, b + 1)
                    wait(act, y_turned, b)
                    for t in range(QB):
                        act.activation(y[:, t, :], x_sub(b, t), ACT.Identity, bias=nmr[:, t:t + 1], scale=rstd[:, t:t + 1]).then_inc(y_ready, 1)

                def squares_of(bank, t, ss, done):
                    for h in range(GROUP):
                        at = slice(h * P, (h + 1) * P)
                        act.activation(squares[:, t, at], bank[:, at], ACT.Square, accum_out=ss[:, t, h:h + 1]).then_inc(done, 1)

                def square_k(f):
                    b = f.b + 1
                    wait(act, k_rs_ready, b)
                    wait(act, q_squared, GROUP * QB * KV * b)
                    for t in range(QB):
                        act.wait_ge(k_sin_done, QB * b + t + 1)
                        squares_of(ring[f.bank("K", KV - 2, t)], t, k_ss, k_squared)

                def square_q(f, g, subs=range(QB)):
                    n = KV * f.b + g + 1
                    if 0 in subs:
                        wait(act, q_rs_ready, n)
                        wait(act, q_squared, GROUP * QB * n)
                        if g == KV - 1:
                            act.wait_ge(k_squared, GROUP * QB * (f.b + 2))
                    for t in subs:
                        act.wait_ge(q_sin_done, QB * n + t + 1)
                        squares_of(ring[f.bank("J", g, t)], t, q_ss, q_squared)

                def exponentials(b, g, h):
                    n = GROUP * (KV * b + g) + h
                    act.wait_ge(bias_ready, n + 1)
                    wait(act, p_turned, n - GROUP + 1)
                    wait(act, inverse_ready, n - GROUP + 1)
                    first = 0
                    for t in range(QB):
                        to = BLOCKS * P if t else P
                        act.activation(prob[:, h, to - SPAN[t]:to], masked[:, h, first:first + SPAN[t]], ACT.Exp,
                                       bias=minus_top[:, h, t:t + 1], scale=q_rs[:, g % 2, t, h:h + 1],
                                       accum_out=total[:, h, t:t + 1]).then_inc(exp_done, 1)
                        first += SPAN[t]

                def high_y(f):
                    b = f.b + 1
                    act.wait_ge(y_turned, b + 1)
                    wait(act, q_projected, QB * KV * b)
                    act.activation(yt_hi[:, :, :], ring[f.bank("Y", KV - 2, 0)][:, :].rearrange("p (k t) -> p k t", k=KC), ACT.Copy).then_inc(yt_hi_ready, 1)

                def high_k(f):
                    b = f.b + 1
                    wait(act, scored, GROUP * KV * b)
                    for t in range(QB):
                        act.wait_ge(k_turned, QB * b + t + 1)
                        act.activation(kt_hi[:, :, t * P:(t + 1) * P], by_head(ring[f.bank("T", KV - 1, t)][:, :]), ACT.Copy).then_inc(kt_hi_ready, 1)

                def high_v(f):
                    wait(act, ctx_summed, QB * KV * f.b)
                    for t in range(QB):
                        act.wait_ge(v_projected, QB * f.b + t + 1)
                        act.activation(v_hi[:, t, :], ring[f.bank("V", 1, t)][:, :], ACT.Copy).then_inc(v_hi_ready, 1)

                def high_q(f, g, subs=range(QB)):
                    n = KV * f.b + g + 1
                    wait(act, scored, GROUP * n)
                    for t in subs:
                        act.wait_ge(q_turned, QB * n + t + 1)
                        act.activation(qt_hi[:, t, :], ring[f.bank("Q", g, t)][:, :], ACT.Copy).then_inc(qt_hi_ready, 1)

                def high_p(f, g, h):
                    n = KV * f.b + g - 1
                    act.wait_ge(p_turned, GROUP * n + h + 1)
                    wait(act, ctx_summed, QB * n)
                    act.activation(pt_hi[:, :, h * P:(h + 1) * P],
                                   ring[f.bank("P", g, h)][:, 0:BLOCKS * P].rearrange("p (k q) -> p k q", k=BLOCKS), ACT.Copy).then_inc(pt_hi_ready, 1)

                def high_c(f, g):
                    n = KV * f.b + g - 2
                    for t in range(QB):
                        act.wait_ge(ctx_summed, QB * n + t + 1)
                        wait(act, projected, QB * (n - 1) + t + 1)
                        act.activation(ctx_hi[:, t, :], ring[f.bank("C", g, t)][:, :], ACT.Copy).then_inc(ctx_hi_ready, 1)

                def slot(b, g):
                    f = Fills(b)
                    here, ahead, turns, sums = stages(b, g)
                    if sums:
                        high_c(f, g)
                    if ahead:
                        square_q(f, g, [0])
                    if turns:
                        high_p(f, g, 0)
                        high_p(f, g, 1)
                        high_p(f, g, 2)
                        high_p(f, g, 3)
                    if ("Y", g, 0) in f.own:
                        high_y(f)
                    if ahead:
                        square_q(f, g, [1])
                    if here:
                        exponentials(b, g, 0)
                        exponentials(b, g, 1)
                        exponentials(b, g, 2)
                        exponentials(b, g, 3)
                    if ("V", g, 0) in f.own:
                        high_v(f)
                        if ahead and stages(b + 1, 0)[0]:
                            normalise(b + 1)
                    if ("K", g, 0) in f.own:
                        square_k(f)
                    if ahead:
                        high_q(f, g)
                    if ("T", g, 0) in f.own:
                        high_k(f)

                f = Fills(-1)
                normalise(0)
                high_y(f)
                square_k(f)
                square_q(f, KV - 1)
                high_k(f)
                high_q(f, KV - 1)
                batches(act, slot)

            @block.vector
            def _(dve):
                def statistics(b):
                    wait(dve, nmr_ready, b)
                    for t in range(QB):
                        dve.bn_stats(stats[:, t, :], x_sub(b, t)).then_inc(stats_done, 1)
                    for t in range(QB):
                        dve.wait_ge(stats_done, QB * b + t + 1)
                        stand(dve)
                        dve.bn_aggr(mv[:, t, :], stats[:, t, :]).then_inc(mv_ready, 1)

                def rope(bank, table, t, by_cos, by_sin, cos_done, sin_done):
                    cos = keep.rope[:, table, 0, t, :]
                    sin = keep.rope[:, table, 1, t, :].rearrange("p (s d) -> p s d", s=2)
                    dve.tensor_tensor(by_head(by_cos[:, t, :]), by_head(bank[:, :]), cos[:, None, :].broadcast_to([P, GROUP, P]), ALU.mult).then_inc(cos_done, 1)
                    dve.tensor_tensor(halves(by_sin[:, t, :]), halves(bank[:, :])[:, :, ::-1, :],
                                      sin[:, None, :, :].broadcast_to([P, GROUP, 2, P // 2]), ALU.mult).then_inc(sin_done, 1)

                def rope_k(f):
                    b = f.b + 1
                    for t in range(QB):
                        dve.wait_ge(k_projected, QB * b + t + 1)
                        wait(dve, k_turned, QB * (b - 1) + t + 1)
                        rope(ring[f.bank("K", KV - 2, t)], 1, t, k_cos, k_sin, k_cos_done, k_sin_done)

                def rope_q(f, g, t):
                    n = KV * f.b + g + 1
                    dve.wait_ge(q_projected, QB * n + t + 1)
                    wait(dve, q_turned, QB * (n - 1) + t + 1)
                    rope(ring[f.bank("J", g, t)], 0, t, q_cos, q_sin, q_cos_done, q_sin_done)

                def maxima(f, g, h):
                    n = GROUP * (KV * f.b + g) + h
                    bank = ring[f.bank("S", g, h)]
                    dve.wait_ge(scored, n + 1)
                    wait(dve, exp_done, QB * (n - GROUP + 1))
                    stand(dve)
                    first = 0
                    for t in range(QB):
                        at = slice(first, first + SPAN[t])
                        dve.tensor_tensor_reduce(masked[:, h, at], bank[:, at], keep.mask[:, at], 1.0, -3e38, ALU.add, ALU.max,
                                                 top[:, h, t:t + 1]).then_inc(top_ready, 1)
                        first += SPAN[t]
                    dve.wait_ge(top_ready, QB * (n + 1))
                    if h == 0:
                        dve.wait_ge(q_rs_ready, KV * f.b + g + 1)
                    dve.scalar_tensor_tensor(minus_top[:, h, :], top[:, h, :], -1.0, q_rs[:, g % 2, :, h], ALU.mult, ALU.mult).then_inc(bias_ready, 1)

                def invert_totals(n, heads):
                    for h in heads:
                        dve.wait_ge(exp_done, QB * (GROUP * n + h + 1))
                        wait(dve, prob_ready, QB * (GROUP * (n - 1) + h + 1))
                        dve.reciprocal(inverse[:, h, :], total[:, h, :]).then_inc(inverse_ready, 1)

                def low(dst, hi, src, done):
                    dve.tensor_tensor(dst, src, hi.bitcast(F32), ALU.subtract).then_inc(done, 1)

                def low_y(f):
                    dve.wait_ge(yt_hi_ready, f.b + 2)
                    low(yt_lo[:, :, :], yt_hi[:, :, :], ring[f.bank("Y", KV - 2, 0)][:, :].rearrange("p (k t) -> p k t", k=KC), yt_ready)

                def low_k(f):
                    for t in range(QB):
                        at = slice(t * P, (t + 1) * P)
                        dve.wait_ge(kt_hi_ready, QB * (f.b + 1) + t + 1)
                        low(kt_lo[:, :, at], kt_hi[:, :, at], by_head(ring[f.bank("T", KV - 1, t)][:, :]), kt_ready)

                def low_v(f):
                    for t in range(QB):
                        dve.wait_ge(v_hi_ready, QB * f.b + t + 1)
                        low(v_lo[:, t, :], v_hi[:, t, :], ring[f.bank("V", 1, t)][:, :], v_ready)

                def low_q(f, g, subs=range(QB)):
                    n = KV * f.b + g + 1
                    for t in subs:
                        dve.wait_ge(qt_hi_ready, QB * n + t + 1)
                        low(qt_lo[:, t, :], qt_hi[:, t, :], ring[f.bank("Q", g, t)][:, :], qt_ready)

                def low_p(f, g, h):
                    at = slice(h * P, (h + 1) * P)
                    dve.wait_ge(pt_hi_ready, GROUP * (KV * f.b + g - 1) + h + 1)
                    low(pt_lo[:, :, at], pt_hi[:, :, at], ring[f.bank("P", g, h)][:, 0:BLOCKS * P].rearrange("p (k q) -> p k q", k=BLOCKS), pt_ready)

                def low_c(f, g):
                    n = KV * f.b + g - 2
                    for t in range(QB):
                        dve.wait_ge(ctx_hi_ready, QB * n + t + 1)
                        low(ctx_lo[:, t, :], ctx_hi[:, t, :], ring[f.bank("C", g, t)][:, :], ctx_ready)

                def add_output(b):
                    dve.wait_ge(projected, QB * KV * (b + 1))
                    at = keep.x[:, bass.ds(b * QB, QB), :].rearrange("p t d -> p (t d)")
                    dve.tensor_tensor(at, out[:, :], at, ALU.add).then_inc(out_used, 1)

                def slot(b, g):
                    f = Fills(b)
                    here, ahead, turns, sums = stages(b, g)
                    if here and g == 0:
                        low_q(Fills(b - 1), KV - 1)
                    if ahead:
                        rope_q(f, g, 0)
                    if here and g == 0:
                        low_k(Fills(b - 1))
                    elif here:
                        low_q(f, g - 1)
                    if sums:
                        low_c(f, g)
                    if g == 2 and sums and not (isinstance(b, int) and b == 0):
                        add_output(b - 1)
                    if turns:
                        low_p(f, g, 0)
                        low_p(f, g, 1)
                    if ahead:
                        rope_q(f, g, 1)
                    if turns:
                        low_p(f, g, 2)
                        low_p(f, g, 3)
                    if ("Y", g, 0) in f.own:
                        low_y(f)
                    if here:
                        maxima(f, g, 0)
                        maxima(f, g, 1)
                        maxima(f, g, 2)
                        maxima(f, g, 3)
                        invert_totals(KV * b + g, (0, 1))
                    if g == 0 and stages(b + 1, 0)[0]:
                        statistics(b + 1)
                    if ("V", g, 0) in f.own:
                        low_v(f)
                    if ("K", g, 0) in f.own:
                        rope_k(f)
                    if here:
                        invert_totals(KV * b + g, (2, 3))

                f = Fills(-1)
                statistics(0)
                low_y(f)
                rope_k(f)
                rope_q(f, KV - 1, 0)
                rope_q(f, KV - 1, 1)
                batches(dve, slot)
                add_output(BATCH - 1)
                dve.wait_ge(out_used, BATCH)

            @block.gpsimd
            def _(pool):
                def rstd_of(b):
                    pool.wait_ge(mv_ready, QB * (b + 1))
                    wait(pool, y_ready, QB * b)
                    stand(pool)
                    pool.tensor_scalar(var[:, :], mv[:, :, 1], 1.0, LN_EPS, ALU.mult, ALU.add).then_inc(var_ready, 1)
                    pool.wait_ge(var_ready, b + 1)
                    pool.tensor_tensor(rstd[:, :], var[:, :], power[:, 0, 0:QB], ALU.pow).then_inc(rstd_ready, 1)
                    pool.wait_ge(rstd_ready, b + 1)
                    pool.tensor_tensor(nmr[:, :], mv[:, :, 0], rstd[:, :], ALU.mult).then_inc(mr_ready, 1)
                    pool.wait_ge(mr_ready, b + 1)
                    stand(pool)
                    pool.tensor_scalar(nmr[:, :], nmr[:, :], -1.0, 1.0, ALU.mult, ALU.mult).then_inc(nmr_ready, 1)

                def add_k(b, t):
                    pool.wait_ge(k_sin_done, QB * b + t + 1)
                    pool.tensor_tensor(k_cos[:, t, :], k_cos[:, t, :], k_sin[:, t, :], ALU.add).then_inc(k_added, 1)

                def rs_of_k(b):
                    pool.wait_ge(k_squared, GROUP * QB * (b + 1))
                    stand(pool)
                    pool.tensor_scalar(k_ms[:, :, :], k_ss[:, :, :], 1.0 / DH, RMS_EPS, ALU.mult, ALU.add).then_inc(k_ms_ready, 1)
                    pool.wait_ge(k_ms_ready, b + 1)
                    pool.tensor_tensor(k_rs[:, :, :], k_ms[:, :, :], power[:, :, :], ALU.pow).then_inc(k_rs_ready, 1)

                def scale_k(b, t):
                    pool.wait_ge(k_rs_ready, b + 1)
                    pool.wait_ge(k_added, QB * b + t + 1)
                    pool.tensor_tensor(by_head(k_cos[:, t, :]), by_head(k_cos[:, t, :]), k_rs[:, t, :, None].broadcast_to([P, KV, DH]), ALU.mult).then_inc(k_normed, 1)

                def add_q(n, t):
                    pool.wait_ge(q_sin_done, QB * n + t + 1)
                    pool.tensor_tensor(q_cos[:, t, :], q_cos[:, t, :], q_sin[:, t, :], ALU.add).then_inc(q_added, 1)

                def norm_q(n, parity):
                    pool.wait_ge(q_squared, GROUP * QB * (n + 1))
                    stand(pool)
                    pool.tensor_scalar(q_ms[:, :, :], q_ss[:, :, :], 1.0, DH * RMS_EPS, ALU.mult, ALU.add).then_inc(q_ms_ready, 1)
                    pool.wait_ge(q_ms_ready, n + 1)
                    wait(pool, exp_done, QB * GROUP * (n - 1))
                    pool.tensor_tensor(q_rs[:, parity, :, :], q_ms[:, :, :], power[:, :, :], ALU.pow).then_inc(q_rs_ready, 1)

                def scale_probs(n, heads):
                    for h in heads:
                        pool.wait_ge(inverse_ready, GROUP * n + h + 1)
                        stand(pool)
                        for t in range(QB):
                            to = BLOCKS * P if t else P
                            at = prob[:, h, to - SPAN[t]:to]
                            pool.tensor_scalar(at, at, inverse[:, h, t:t + 1], 1.0, ALU.mult, ALU.mult).then_inc(prob_ready, 1)

                def slot(b, g):
                    f = Fills(b)
                    here, ahead, turns, sums = stages(b, g)
                    n = KV * b + g
                    if ahead:
                        add_q(n + 1, 0)
                    if ("T", g, 0) in f.own:
                        rs_of_k(b + 1)
                        scale_k(b + 1, 0)
                    if ahead:
                        add_q(n + 1, 1)
                    if ("T", g, 0) in f.own:
                        scale_k(b + 1, 1)
                    if ahead:
                        norm_q(n + 1, (g + 1) % 2)
                    if ("V", g, 0) in f.own and stages(b + 1, 0)[0]:
                        rstd_of(b + 1)
                    if here:
                        scale_probs(n, (0, 1))
                    if ("K", g, 0) in f.own:
                        add_k(b + 1, 0)
                        add_k(b + 1, 1)
                    if here:
                        scale_probs(n, (2, 3))

                pool.memset(power[:, :, :], -0.5).then_inc(set_up, 1)
                pool.memset(prob[:, :, P:2 * P], 0.0).then_inc(set_up, 1)
                pool.wait_ge(set_up, 2)
                rstd_of(0)
                add_k(0, 0)
                add_k(0, 1)
                rs_of_k(0)
                scale_k(0, 0)
                scale_k(0, 1)
                add_q(0, 0)
                add_q(0, 1)
                norm_q(0, 0)
                batches(pool, slot)


class Kept:

    def __init__(self, nc, stack):
        def sb(name, shape, dt):
            return stack.enter_context(nc.sbuf_tensor(name, shape, dt))

        self.x = sb("x", [P, SUB, D], F32)
        with ExitStack() as early:
            self.early = [early.enter_context(nc.sbuf_tensor(name, shape, F32)) for name, shape in (
                ("raw8", [P, M, 3 * D]), ("magic", [P, 2, 3 * D]), ("q8", [P, 2, 3 * D]), ("over", [P, 2, 3 * D]),
                ("raw_scale", [P, 2, M]), ("down_s", [P, D]), ("wrow", [P, 2, DH]), ("rope_raw", [P, 2, 2, DH]))]
        self.wqkv_hi = sb("wqkv_hi", [P, KC, QKV], F32R)
        self.wqkv_lo = sb("wqkv_lo", [P, KC, QKV], F32R)
        self.wo_hi = sb("wo_hi", [P, HEADS * D], F32R)
        self.wo_lo = sb("wo_lo", [P, HEADS * D], F32R)
        self.w8 = sb("w8", [P, M, 3 * D], BF16)
        self.gate_half = sb("gate_half", [P, M], F32)
        self.gate_up = sb("gate_up", [P, M], F32)
        self.down_half = sb("down_half", [P, D], F32)
        self.rope = sb("rope", [P, 2, 2, 2, DH], F32)
        self.ident = sb("ident", [P, P], F32)
        self.mask = sb("mask", [P, 2 * P + WINDOW], F32)


def build(nc, dram, out):
    with ExitStack() as stack:
        keep = Kept(nc, stack)
        ffn_phase(nc, stack, keep, "f_", dram=dram)
        attention_phase(nc, stack, keep)
        ffn_phase(nc, stack, keep, "g_", out_dram=out)


def constants():
    inv_freq = (1.0 / np.float32(10000.0) ** (np.arange(0, DH, 2, dtype=np.float32) / np.float32(DH))).astype(np.float32)
    freqs = np.arange(T, dtype=np.float32)[:, None] * inv_freq[None, :]
    cos, sin = np.cos(freqs), np.sin(freqs)
    q, k0, k1 = np.arange(P)[:, None], np.arange(P)[None, :], np.arange(-WINDOW, P)[None, :]
    seen = np.concatenate([(q >= k0) & (q - k0 <= WINDOW), (q >= k1) & (q - k1 <= WINDOW)], axis=1)
    return {
        "cos": np.concatenate([cos, cos], axis=1),
        "sin": np.concatenate([-sin, sin], axis=1),
        "mask": np.where(seen, np.float32(0), np.float32(MASKED)),
        "ident": np.eye(P, dtype=np.float32),
    }


def kernel(L0_attn_x, L0_attn_Wq, L0_attn_Wk, L0_attn_Wv, L0_attn_Wo, L0_attn_qn_w, L0_attn_kn_w,
           L0_ffn_gate_w, L0_ffn_up_w, L0_ffn_down_w, L0_ffn_gate_scale, L0_ffn_up_scale, L0_ffn_down_scale):
    import concourse.bacc as bacc
    from concourse.bass_utils import run_bass_kernel_spmd

    given = {
        "x": L0_attn_x,
        "wqkv_t": np.concatenate([L0_attn_Wq, L0_attn_Wk, L0_attn_Wv], axis=0).T,
        "wo_t": np.asarray(L0_attn_Wo).T,
        "qn": L0_attn_qn_w, "kn": L0_attn_kn_w,
        "gate_w": L0_ffn_gate_w, "up_w": L0_ffn_up_w, "down_w": L0_ffn_down_w,
        "gate_s": np.asarray(L0_ffn_gate_scale).reshape(M, P).T, "up_s": np.asarray(L0_ffn_up_scale).reshape(M, P).T, "down_s": L0_ffn_down_scale,
    }
    given.update(constants())
    nc = bacc.Bacc("TRN2", target_bir_lowering=False, num_devices=1)
    arrays, dram = {}, {}
    for name, a in given.items():
        a = np.ascontiguousarray(a)
        arrays[f"in_{name}"] = a
        dram[name] = nc.dram_tensor(f"in_{name}", a.shape, mybir.dt.from_np(a.dtype), kind="ExternalInput").ap()
    out = nc.dram_tensor("out", (BATCH, T, D), F32, kind="ExternalOutput").ap()
    build(nc, dram, out)
    return run_bass_kernel_spmd(nc, [arrays], core_ids=[0]).results[0]["out"]
```

```python
from contextlib import ExitStack

import numpy as np

import concourse.bass as bass
from concourse import mybir

ALU = mybir.AluOpType
ACT = mybir.ActivationFunctionType
F32 = mybir.dt.float32
F32R = mybir.dt.float32r
BF16 = mybir.dt.bfloat16
I32 = mybir.dt.int32

P = 128
BATCH, T, D = 16, 256, 256
HEADS, KV, DH = 16, 4, 128
GROUP = HEADS // KV
WINDOW = 64
I = 768
KC = D // P
M = I // P
SUB = BATCH * T // P
FFN_SUBS = 4
QKV = (HEADS + 2 * KV) * DH
LN_EPS = 1e-5
RMS_EPS = 1e-6
MASKED = -1e30

F8_MIN_NORMAL = 2.0 ** -6
F8_MAGIC = 1.5 * 2.0 ** 20
F8_OVER = float(np.float32(2.0 ** 119 * 512 / 464))


class Phase:

    def __init__(self, nc, stack, semaphores, prefix):
        self.nc, self.stack, self.semaphores, self.prefix = nc, stack, semaphores, prefix

    def sb(self, name, shape, dt):
        return self.stack.enter_context(self.nc.sbuf_tensor(self.prefix + name, shape, dt))

    def ps(self, name, shape=(P, 512), dt=F32):
        return self.stack.enter_context(self.nc.psum_tensor(self.prefix + name, list(shape), dt))

    def sem(self, name):
        return self.semaphores.enter_context(self.nc.semaphore(self.prefix + name))


def stand(eng):
    eng.nop(nofuse=True)


def wait(eng, sem, value):
    if not isinstance(value, int) or value > 0:
        eng.wait_ge(sem, value)


def product(pe, out, parts, start=True, stop=True):
    for n, (w, x) in enumerate(parts):
        last = pe.matmul(out, w, x, start=start and n == 0, stop=stop and n == len(parts) - 1,
                         skip_group_check=True)
    return last


def three(w_hi, w_lo, x_hi, x_lo):
    return [(w_hi, x_hi), (w_hi, x_lo), (w_lo, x_hi)]


class Norm:

    def __init__(self, nc, semaphores, keep, prefix, subs):
        self.keep, self.subs = keep, subs

        def sem(name):
            return semaphores.enter_context(nc.semaphore(prefix + name))

        self.stats_done = sem("stats_done")
        self.mv_ready = sem("mv_ready")
        self.var_ready = sem("var_ready")
        self.rstd_ready = sem("rstd_ready")
        self.mr_ready = sem("mr_ready")
        self.nmr_ready = sem("nmr_ready")
        self.y_ready = sem("y_ready")

    def x_sub(self, t, s):
        return self.keep.x[:, bass.ds(t * self.subs + s, 1), :].rearrange("p a d -> p (a d)")

    def statistics(self, dve, t):
        keep = self.keep
        wait(dve, self.nmr_ready, t)
        for s in range(self.subs):
            dve.bn_stats(keep.stats[:, s, :], self.x_sub(t, s)).then_inc(self.stats_done, 1)
        for s in range(self.subs):
            dve.wait_ge(self.stats_done, self.subs * t + s + 1)
            stand(dve)
            dve.bn_aggr(keep.mv[:, s, :], keep.stats[:, s, :]).then_inc(self.mv_ready, 1)

    def rstd_of(self, pool, t):
        at, keep = slice(0, self.subs), self.keep
        pool.wait_ge(self.mv_ready, self.subs * (t + 1))
        wait(pool, self.y_ready, self.subs * t)
        stand(pool)
        pool.tensor_scalar(keep.var[:, at], keep.mv[:, at, 1], 1.0, LN_EPS, ALU.mult, ALU.add).then_inc(self.var_ready, 1)
        pool.wait_ge(self.var_ready, t + 1)
        pool.tensor_tensor(keep.rstd[:, at], keep.var[:, at], keep.power[:, 0, at], ALU.pow).then_inc(self.rstd_ready, 1)
        pool.wait_ge(self.rstd_ready, t + 1)
        pool.tensor_tensor(keep.nmr[:, at], keep.mv[:, at, 0], keep.rstd[:, at], ALU.mult).then_inc(self.mr_ready, 1)
        pool.wait_ge(self.mr_ready, t + 1)
        stand(pool)
        pool.tensor_scalar(keep.nmr[:, at], keep.nmr[:, at], -1.0, 1.0, ALU.mult, ALU.mult).then_inc(self.nmr_ready, 1)

    def normalise(self, act, t, subs):
        keep = self.keep
        act.wait_ge(self.nmr_ready, t + 1)
        for s in subs:
            act.activation(keep.y[:, s, :], self.x_sub(t, s), ACT.Identity,
                           bias=keep.nmr[:, s:s + 1], scale=keep.rstd[:, s:s + 1]).then_inc(self.y_ready, 1)


def ffn_phase(nc, semaphores, keep, prefix, norm, next_norm=None, dram=None, out_dram=None):
    SUBS = FFN_SUBS
    TILE = SUBS * P
    TILES = BATCH * T // TILE
    GU_AHEAD = 3
    SPLIT = 4
    EARLY = 4
    CH = 512
    RAW = 4
    LOW_AT = {1: [3, 3, 4, 4, 5, 5], TILES - 2: [1, 3, 3, 4, 4, 5, 5], TILES - 1: [1, 2, 2, 3, 3, 4, 4]}
    assert sum(len(steps) for steps in LOW_AT.values()) == (KC * QKV + HEADS * D) // CH
    with ExitStack() as stack:
        ph = Phase(nc, stack, semaphores, prefix)
        w8 = ph.sb("w8", [P, M, 3 * D], F32R)
        yt_hi = ph.sb("yt_hi", [P, 2, KC, TILE], F32R)
        yt_lo = ph.sb("yt_lo", [P, 2, KC, TILE], F32R)
        th = ph.sb("th", [P, 2, TILE], F32)
        gated = ph.sb("gated", [P, 2, TILE], F32)
        h = ph.sb("h", [P, 2, TILE], F32)
        h_hi = ph.sb("h_hi", [P, SPLIT, TILE], F32R)
        h_lo = ph.sb("h_lo", [P, SPLIT, TILE], F32R)
        scaled = ph.sb("scaled", [P, 2, TILE], F32)

        if dram:
            raw = ph.sb("raw", [P, RAW, CH], F32)
            raw_loaded = [ph.sem(f"raw_loaded{k}") for k in range(RAW)]
            raw8, magic, q8, over, raw_scale, down_s, wrow, rope_raw = keep.early
            x_loaded = [ph.sem(f"x_loaded{t}") for t in range(TILES)]
            ffn_loaded = [ph.sem(f"ffn_loaded{m}") for m in range(M)]
            scales_loaded = ph.sem("scales_loaded")
            down_s_loaded = ph.sem("down_s_loaded")
            ident_loaded = ph.sem("ident_loaded")
            rope_loaded = ph.sem("rope_loaded")
            mask_loaded = ph.sem("mask_loaded")
            exponent = ph.sem("exponent")
            magic_ready = ph.sem("magic_ready")
            added = ph.sem("added")
            rounded = ph.sem("rounded")
            scaled_over = ph.sem("scaled_over")
            over_ready = ph.sem("over_ready")
            w8_kept = ph.sem("w8_kept")
            scales_ready = ph.sem("scales_ready")
            one_plus = ph.sem("one_plus")
            rope_ready = ph.sem("rope_ready")
            raw_hi = ph.sem("raw_hi")
            raw_split = ph.sem("raw_split")

        def chunks():
            wqkv = dram["wqkv_t"].rearrange("(k p) n -> p k n", p=P)
            wo = dram["wo_t"].rearrange("(h p) n -> p h n", p=P)
            found = []
            for k in range(KC):
                for c in range(QKV // CH):
                    at = slice(c * CH, (c + 1) * CH)
                    found.append((wqkv[:, k, at], keep.wqkv_hi[:, k, at], keep.wqkv_lo[:, k, at]))
            for c in range(HEADS * D // CH):
                at = slice(c * CH, (c + 1) * CH)
                heads = slice(c * CH // D, (c + 1) * CH // D)
                found.append((wo[:, heads, :], keep.wo_hi[:, at], keep.wo_lo[:, at]))
            return found

        gate = [ph.ps(f"gate{k}") for k in range(2)]
        up = [ph.ps(f"up{k}") for k in range(2)]
        turn = [ph.ps(f"turn{k}") for k in range(KC)]
        acc = [ph.ps(f"acc{k}") for k in range(2)]

        w8_ready = ph.sem("w8_ready")
        power_set = ph.sem("power_set")
        w8_rest_ready = ph.sem("w8_rest_ready")
        turned = ph.sem("turned")
        yt_hi_ready = ph.sem("yt_hi_ready")
        yt_ready = ph.sem("yt_ready")
        gate_ready = ph.sem("gate_ready")
        up_ready = ph.sem("up_ready")
        th_ready = ph.sem("th_ready")
        gate_used = ph.sem("gate_used")
        h_ready = ph.sem("h_ready")
        h_hi_ready = ph.sem("h_hi_ready")
        h_split = ph.sem("h_split")
        down_done = ph.sem("down_done")
        acc_used = ph.sem("acc_used")
        x_done = ph.sem("x_done")
        stored = ph.sem("stored")

        def h_place(t, parity, m):
            return (parity * M + m) % SPLIT

        def norm_late(t):
            return bool(dram) and isinstance(t, int) and t == 0

        def chunks_of_step(t, m):
            if not dram or not isinstance(t, int):
                return []
            before = sum(len(steps) for tile, steps in LOW_AT.items() if tile < t)
            return [before + n for n, at in enumerate(LOW_AT.get(t, [])) if at == m]

        def pairs(eng, tile):
            tile(0, 0, 0, 2)
            tile(1, 1, 1, 2)
            with eng.Fori(1, TILES // 2 - 1) as pair:
                tile(2 * pair, 0, 2, 2)
                tile(2 * pair + 1, 1, 2, 2)
            tile(TILES - 2, 0, 2, 1)
            tile(TILES - 1, 1, 2, 0)

        def x_of(t):
            return keep.x[:, bass.ds(t * SUBS, SUBS), :]

        def load_x(eng, t):
            x_in = dram["x"].rearrange("b (t p) d -> p (b t) d", p=P)
            eng.dma_start(x_of(t), x_in[:, t * SUBS:(t + 1) * SUBS, :]).then_inc(x_loaded[t], 16)

        def add_to_x(eng, t, k):
            eng.wait_ge(acc_used, 2 * t + k + 1)
            at = keep.x[:, bass.ds(t * SUBS + 2 * k, 2), :].rearrange("p s d -> p (s d)")
            eng.tensor_tensor(at, at, scaled[:, k, :], ALU.add).then_inc(x_done, 1)

        with nc.Block() as block:

            @block.tensor
            def _(pe):
                def turn_y(t):
                    pe.wait_ge(norm.y_ready, SUBS * (t + 1))
                    wait(pe, yt_ready, KC * t)
                    for k in range(KC):
                        for s in range(SUBS):
                            last = pe.transpose(turn[k][:, s * P:(s + 1) * P], keep.y[:, s, k * P:(k + 1) * P], keep.ident[:, :])
                        last.then_inc(turned, 1)

                def gate_up(t, parity, m):
                    step = t * M + m
                    if dram and isinstance(t, int) and t == 0:
                        pe.wait_ge(w8_ready, m + 1)
                    elif isinstance(t, int) and t == 0 and m == 0:
                        pe.wait_ge(w8_ready, 1)
                    elif isinstance(t, int) and t == 0 and m == M // 2:
                        pe.wait_ge(w8_rest_ready, 1)
                    if m == 0:
                        pe.wait_ge(yt_ready, KC * (t + 1))
                    wait(pe, gate_used, step - 1)
                    for a, (bank, ready) in enumerate(((gate[m % 2], gate_ready), (up[m % 2], up_ready))):
                        if a:
                            wait(pe, h_ready, step - 1)
                        parts = []
                        for k in range(KC):
                            w = w8[:, m, a * D + k * P:a * D + (k + 1) * P]
                            parts += [(w, yt_hi[:, parity, k, :]), (w, yt_lo[:, parity, k, :])]
                        product(pe, bank[:, :], parts).then_inc(ready, 1)

                def down(t, parity, m):
                    step = t * M + m
                    pe.wait_ge(h_split, step + 1)
                    place = h_place(t, parity, m)
                    if m == 0:
                        wait(pe, acc_used, 2 * t)
                    w = w8[:, m, 2 * D:]
                    for s in range(SUBS):
                        at = slice(s * P, (s + 1) * P)
                        out = acc[s // 2][:, (s % 2) * D:(s % 2 + 1) * D]
                        last = product(pe, out, [(h_hi[:, place, at], w), (h_lo[:, place, at], w)],
                                       start=(m == 0 and s % 2 == 0), stop=(m == M - 1))
                    last.then_inc(down_done, 1)

                def tile(t, parity, before, after):
                    for m in range(M):
                        if m + GU_AHEAD < M:
                            gate_up(t, parity, m + GU_AHEAD)
                        elif after:
                            gate_up(t + 1, 1 - parity, m + GU_AHEAD - M)
                        down(t, parity, m)
                        if m == 0 and after:
                            turn_y(t + 1)

                if dram:
                    pe.wait_ge(ident_loaded, 16)
                turn_y(0)
                for m in range(GU_AHEAD):
                    gate_up(0, 0, m)
                pairs(pe, tile)

            @block.scalar
            def _(act):
                def normalise(t, subs):
                    wait(act, turned, KC * t)
                    norm.normalise(act, t, subs)

                def yt_high(t, parity):
                    for k in range(KC):
                        act.wait_ge(turned, KC * t + k + 1)
                        if k == 0:
                            wait(act, up_ready, M * (t - 1))
                        act.activation(yt_hi[:, parity, k, :], turn[k][:, :], ACT.Copy).then_inc(yt_hi_ready, 1)

                def tanh(t, m):
                    step = t * M + m
                    act.wait_ge(gate_ready, step + 1)
                    wait(act, gate_used, step - 1)
                    act.activation(th[:, m % 2, :], gate[m % 2][:, :], ACT.Tanh, scale=keep.gate_half[:, m:m + 1]).then_inc(th_ready, 1)

                def tile(t, parity, before, after):
                    for m in range(M):
                        step = t * M + m
                        if m + 1 < M:
                            tanh(t, m + 1)
                        elif after:
                            tanh(t + 1, 0)
                        act.wait_ge(h_ready, step + 1)
                        wait(act, down_done, step - SPLIT + 1)
                        act.activation(h_hi[:, h_place(t, parity, m), :], h[:, m % 2, :], ACT.Copy).then_inc(h_hi_ready, 1)
                        first = dram and isinstance(t, int) and t == 0
                        if first and m >= M // 2:
                            for k in (2 * m - M, 2 * m - M + 1):
                                act.wait_ge(w8_ready, k + 1)
                                act.activation(keep.w8[:, k, :], w8[:, k, :].bitcast(F32), ACT.Copy).then_inc(w8_kept, 1)
                        for n in chunks_of_step(t, m + 1):
                            if n == 0:
                                act.wait_ge(w8_ready, M)
                                act.wait_ge(scales_ready, 3)
                                act.wait_ge(rope_ready, 8)
                            act.wait_ge(raw_loaded[n % RAW], 16 * (n // RAW + 1))
                            act.activation(chunks()[n][1], raw[:, n % RAW, :], ACT.Copy).then_inc(raw_hi, 1)
                        if m == 2 and after:
                            yt_high(t + 1, 1 - parity)
                        if first and m + EARLY < M:
                            overflow(m + EARLY)
                        if m == 5 and after == 2 and norm_late(t):
                            normalise(t + 2, range(SUBS))
                        if next_norm and m == 4 and not after:
                            act.wait_ge(turned, KC * TILES)
                            next_norm.normalise(act, 0, range(next_norm.subs))
                        elif m in (4, 5) and after == 2 and not norm_late(t):
                            normalise(t + 2, range(2 * (m - 4), 2 * (m - 3)))

                def overflow(m):
                    act.wait_ge(rounded, m + 1)
                    wait(act, w8_ready, m - 1)
                    act.activation(over[:, m % 2, :], q8[:, m % 2, :], ACT.Copy, scale=F8_OVER).then_inc(scaled_over, 1)
                    act.wait_ge(scaled_over, m + 1)
                    act.activation(over[:, m % 2, :], over[:, m % 2, :], ACT.Copy, scale=0.0).then_inc(over_ready, 1)

                if dram:
                    load_x(act, 0)
                    act.dma_start(keep.ident[:, :], dram["ident"]).then_inc(ident_loaded, 16)
                    act.dma_start(raw_scale[:, 0, :], dram["gate_s"]).then_inc(scales_loaded, 16)
                    act.dma_start(raw_scale[:, 1, :], dram["up_s"]).then_inc(scales_loaded, 16)
                    load_x(act, 1)
                    normalise(0, range(SUBS))
                    overflow(0)
                    yt_high(0, 0)
                    for m in range(1, EARLY):
                        overflow(m)
                else:
                    yt_high(0, 0)
                    normalise(1, range(SUBS))
                if dram:
                    act.wait_ge(scales_ready, 2)
                tanh(0, 0)
                if dram:
                    normalise(1, range(SUBS))
                else:
                    act.activation(w8[:, M // 2:, :], keep.w8[:, M // 2:, :], ACT.Copy).then_inc(w8_rest_ready, 1)
                pairs(act, tile)

            @block.vector
            def _(dve):
                def statistics(t):
                    if dram and isinstance(t, int) and t < 4:
                        for part in range(t, t + 1 if t < 3 else TILES):
                            dve.wait_ge(x_loaded[part], 16)
                    norm.statistics(dve, t)

                def yt_low(t, parity):
                    for k in range(KC):
                        dve.wait_ge(yt_hi_ready, KC * t + k + 1)
                        dve.tensor_tensor(yt_lo[:, parity, k, :], turn[k][:, :], yt_hi[:, parity, k, :].bitcast(F32), ALU.subtract).then_inc(yt_ready, 1)

                def scale_sums(t):
                    dve.wait_ge(down_done, M * (t + 1))
                    if dram and isinstance(t, int) and t == 0:
                        dve.wait_ge(scales_ready, 3)
                    wait(dve, x_done, 2 * t)
                    for k in range(2):
                        scale = keep.down_half[:, None, :].broadcast_to([P, 2, D])
                        dve.tensor_tensor(scaled[:, k, :].rearrange("p (s d) -> p s d", d=D), acc[k][:, :].rearrange("p (s d) -> p s d", d=D),
                                          scale, ALU.mult).then_inc(acc_used, 1)

                def tile(t, parity, before, after):
                    for m in range(M):
                        step = t * M + m
                        dve.wait_ge(th_ready, step + 1)
                        dve.scalar_tensor_tensor(gated[:, m % 2, :], th[:, m % 2, :], 1.0, gate[m % 2][:, :], ALU.add, ALU.mult).then_inc(gate_used, 1)
                        dve.wait_ge(up_ready, step + 1)
                        dve.wait_ge(gate_used, step + 1)
                        wait(dve, h_split, step - 1)
                        dve.scalar_tensor_tensor(h[:, m % 2, :], up[m % 2][:, :], keep.gate_up[:, m:m + 1], gated[:, m % 2, :], ALU.mult, ALU.mult).then_inc(h_ready, 1)
                        if m == 1 and before:
                            scale_sums(t - 1)
                        if m == 2 and after:
                            yt_low(t + 1, 1 - parity)
                        if next_norm and m == 0 and not after:
                            dve.wait_ge(norm.nmr_ready, TILES)
                            dve.wait_ge(x_done, 2)
                            next_norm.statistics(dve, 0)
                        if m == (4 if norm_late(t) else 0) and after == 2:
                            statistics(t + 2)
                        first = dram and isinstance(t, int) and t == 0
                        if first and m + EARLY < M:
                            round_weights(m + EARLY)
                        if dram and isinstance(t, int) and t == 1 and m == 0:
                            rope_tables()
                        for n in chunks_of_step(t, m):
                            hi, lo = chunks()[n][1:]
                            dve.wait_ge(raw_hi, n + 1)
                            dve.tensor_tensor(lo, raw[:, n % RAW, :], hi.bitcast(F32), ALU.subtract).then_inc(raw_split, 1)

                def round_weights(m):
                    w, mg, q = raw8[:, m, :], magic[:, m % 2, :], q8[:, m % 2, :]
                    dve.wait_ge(ffn_loaded[m], 16 * 3)
                    wait(dve, rounded, m - 1)
                    dve.tensor_scalar(mg.bitcast(I32), w.bitcast(I32), 0x7F800000, None, ALU.bitwise_and).then_inc(exponent, 1)
                    dve.wait_ge(exponent, m + 1)
                    dve.tensor_scalar(mg, mg, F8_MIN_NORMAL, F8_MAGIC, ALU.max, ALU.mult).then_inc(magic_ready, 1)
                    dve.wait_ge(magic_ready, m + 1)
                    dve.tensor_tensor(w, w, mg, ALU.add).then_inc(added, 1)
                    dve.wait_ge(added, m + 1)
                    wait(dve, w8_ready, m - 1)
                    dve.tensor_tensor(q, w, mg, ALU.subtract).then_inc(rounded, 1)

                def scale_tables():
                    dve.wait_ge(scales_loaded, 16 * 2)
                    dve.tensor_scalar(keep.gate_half[:, :], raw_scale[:, 0, :], 0.5, None, ALU.mult).then_inc(scales_ready, 1)
                    dve.scalar_tensor_tensor(keep.gate_up[:, :], raw_scale[:, 0, :], 0.5, raw_scale[:, 1, :], ALU.mult, ALU.mult).then_inc(scales_ready, 1)

                def rope_tables():
                    dve.wait_ge(down_s_loaded, 16)
                    dve.tensor_scalar(keep.down_half[:, :], down_s[:, :], 0.5, None, ALU.mult).then_inc(scales_ready, 1)
                    dve.wait_ge(rope_loaded, 16 * 4)
                    dve.tensor_scalar(wrow[:, :, :], wrow[:, :, :], 1.0, None, ALU.add).then_inc(one_plus, 1)
                    dve.wait_ge(one_plus, 1)
                    for n in range(2):
                        w = wrow[:, n, :]
                        swapped = w.rearrange("p (s d) -> p s d", s=2)[:, ::-1, :]
                        for t in range(2):
                            dve.tensor_tensor(keep.rope[:, n, 0, t, :], rope_raw[:, 0, t, :], w, ALU.mult).then_inc(rope_ready, 1)
                            dve.tensor_tensor(keep.rope[:, n, 1, t, :].rearrange("p (s d) -> p s d", s=2),
                                              rope_raw[:, 1, t, :].rearrange("p (s d) -> p s d", s=2), swapped, ALU.mult).then_inc(rope_ready, 1)

                if dram:
                    statistics(0)
                    round_weights(0)
                    scale_tables()
                    round_weights(1)
                    yt_low(0, 0)
                    for m in range(2, EARLY):
                        round_weights(m)
                    statistics(1)
                    dve.wait_ge(scales_ready, 2)
                else:
                    dve.tensor_copy(w8[:, 0:M // 2, :], keep.w8[:, 0:M // 2, :]).then_inc(w8_ready, 1)
                    yt_low(0, 0)
                pairs(dve, tile)
                scale_sums(TILES - 1)
                add_to_x(dve, TILES - 1, 1)

            @block.gpsimd
            def _(pool):
                def finish_weights(m):
                    pool.wait_ge(over_ready, m + 1)
                    pool.tensor_tensor(w8[:, m, :], q8[:, m % 2, :], over[:, m % 2, :], ALU.add).then_inc(w8_ready, 1)

                def tile(t, parity, before, after):
                    for m in range(M):
                        step = t * M + m
                        pool.wait_ge(h_hi_ready, step + 1)
                        place = h_place(t, parity, m)
                        pool.tensor_tensor(h_lo[:, place, :], h[:, m % 2, :], h_hi[:, place, :].bitcast(F32), ALU.subtract).then_inc(h_split, 1)
                        if dram and isinstance(t, int) and t == 0 and m + EARLY < M:
                            finish_weights(m + EARLY)
                        if m in (1, 2) and before:
                            add_to_x(pool, t - 1, m - 1)
                        if next_norm and m == 2 and not after:
                            pool.wait_ge(norm.y_ready, SUBS * TILES)
                            next_norm.rstd_of(pool, 0)
                        if m == (4 if norm_late(t) else 3) and after == 2:
                            norm.rstd_of(pool, t + 2)

                if dram:
                    pool.memset(keep.power[:, :, :], -0.5).then_inc(power_set, 1)
                    pool.wait_ge(power_set, 1)
                    norm.rstd_of(pool, 0)
                    for m in range(EARLY):
                        finish_weights(m)
                    norm.rstd_of(pool, 1)
                pairs(pool, tile)
                add_to_x(pool, TILES - 1, 0)

            @block.sync
            def _(sp):
                if dram:
                    gate_w = dram["gate_w"].rearrange("(k p) (m i) -> m p k i", p=P, i=P)
                    up_w = dram["up_w"].rearrange("(k p) (m i) -> m p k i", p=P, i=P)
                    down_w = dram["down_w"].rearrange("(m p) d -> m p d", p=P)
                    for m in range(M):
                        three_w = raw8[:, m, :].rearrange("p (a k i) -> p a k i", a=3, k=KC)
                        sp.dma_start(three_w[:, 0], gate_w[m]).then_inc(ffn_loaded[m], 16)
                        sp.dma_start(three_w[:, 1], up_w[m]).then_inc(ffn_loaded[m], 16)
                        sp.dma_start(raw8[:, m, 2 * D:], down_w[m]).then_inc(ffn_loaded[m], 16)
                        if m == GU_AHEAD:
                            sp.dma_start(down_s[:, :], dram["down_s"].partition_broadcast(P)).then_inc(down_s_loaded, 16)
                            load_x(sp, 2)
                    for t in range(3, TILES):
                        load_x(sp, t)
                    sp.dma_start(wrow[:, 0, :], dram["qn"].partition_broadcast(P)).then_inc(rope_loaded, 16)
                    sp.dma_start(wrow[:, 1, :], dram["kn"].partition_broadcast(P)).then_inc(rope_loaded, 16)
                    sp.dma_start(rope_raw[:, 0], dram["cos"].rearrange("(t p) d -> p t d", p=P)).then_inc(rope_loaded, 16)
                    sp.dma_start(rope_raw[:, 1], dram["sin"].rearrange("(t p) d -> p t d", p=P)).then_inc(rope_loaded, 16)
                    sp.dma_start(keep.mask[:, :], dram["mask"]).then_inc(mask_loaded, 16)
                    for n, (src, _hi, _lo) in enumerate(chunks()):
                        if n >= RAW:
                            sp.wait_ge(raw_split, n - RAW + 1)
                        place = raw[:, n % RAW, :]
                        if n >= KC * QKV // CH:
                            place = place.rearrange("p (h n) -> p h n", n=D)
                        sp.dma_start(place, src).then_inc(raw_loaded[n % RAW], 16)
                    sp.wait_ge(mask_loaded, 16)
                if out_dram is not None:
                    view = out_dram.rearrange("b (t p) d -> p (b t) d", p=P)
                    with sp.Fori(0, TILES) as t:
                        sp.wait_ge(x_done, 2 * t + 2)
                        sp.dma_start(view[:, bass.ds(t * SUBS, SUBS), :], x_of(t)).then_inc(stored, 16)
                    sp.wait_ge(stored, 16 * TILES)


RING = 7


def stages(b, g):
    if not isinstance(b, int):
        return True, True, True, True
    n, end = KV * b + g, KV * BATCH
    return n < end, n + 1 < end, 1 <= n <= end, n >= 2


def fills_of_batch(b):
    fills = []
    for g in range(KV if b < BATCH else 2):
        here, ahead, turns, sums = stages(b, g)
        two = [0, 1]
        order = [("J", [0], ahead), ("C", two, sums), ("P", [0, 1], turns), ("J", [1], ahead), ("P", [2, 3], turns),
                 ("Y", [0], ahead and g == KV - 2 and b < BATCH - 1), ("S", range(GROUP), here),
                 ("V", two, here and g == 1), ("K", two, here and g == KV - 2 and b < BATCH - 1),
                 ("Q", two, ahead), ("T", two, ahead and g == KV - 1)]
        fills += [(what, g, part) for what, parts, used in order if used for part in parts]
    return fills


BEFORE = [("Y", KV - 2, 0), ("K", KV - 2, 0), ("K", KV - 2, 1)] + [(what, KV - 1, t) for what in "JTQ" for t in range(2)]
FIRST, STEADY, LAST, AFTER = (fills_of_batch(b) for b in (0, 1, BATCH - 1, BATCH))
assert len(STEADY) % RING == 0 and FIRST[-RING:] == STEADY[-RING:]


class Fills:

    def __init__(self, b):
        self.b = b
        at = b if isinstance(b, int) else 1
        steady = len(BEFORE) + len(FIRST)
        self.own = {-1: BEFORE, 0: FIRST, BATCH - 1: LAST, BATCH: AFTER}.get(at, STEADY)
        self.former = {-1: [], 0: BEFORE, BATCH: LAST}.get(at, STEADY)
        self.start = {-1: 0, 0: len(BEFORE), BATCH: steady + len(LAST)}.get(at, steady)

    def bank(self, what, g, part):
        return (self.start + self.own.index((what, g, part))) % RING

    def contents_before(self, what, g, part):
        n = self.own.index((what, g, part)) - RING
        if n >= 0:
            return self.own[n], self.b
        return (self.former[n], self.b - 1) if self.former else None


def attention_phase(nc, semaphores, keep, norm, next_norm):
    QB = T // P
    SPAN = [P, P + WINDOW]
    SPANS = sum(SPAN)
    BLOCKS = 3
    QUERIES = [P, WINDOW, P]
    Q_AT = [0, P, P + WINDOW]
    QS = sum(QUERIES)
    HW = GROUP * P
    K_AT, V_AT = HEADS * DH, (HEADS + KV) * DH
    with ExitStack() as stack:
        ph = Phase(nc, stack, semaphores, "a_")
        yt_hi = ph.sb("yt_hi", [P, KC, T], F32R)
        yt_lo = ph.sb("yt_lo", [P, KC, T], F32R)
        q_cos = ph.sb("q_cos", [P, QB, HW], F32)
        k_cos = ph.sb("k_cos", [P, QB, HW], F32)
        q_sin = ph.sb("q_sin", [P, QB, HW], F32)
        k_sin = ph.sb("k_sin", [P, QB, HW], F32)
        q_ss = ph.sb("q_ss", [P, QB, GROUP], F32)
        k_ss = ph.sb("k_ss", [P, QB, KV], F32)
        q_ms = ph.sb("q_ms", [P, QB, GROUP], F32)
        k_ms = ph.sb("k_ms", [P, QB, KV], F32)
        q_rs = ph.sb("q_rs", [P, 2, QB, GROUP], F32)
        k_rs = ph.sb("k_rs", [P, QB, KV], F32)
        qt_hi = ph.sb("qt_hi", [P, QB, HW], F32R)
        qt_lo = ph.sb("qt_lo", [P, QB, HW], F32R)
        kt_hi = ph.sb("kt_hi", [P, KV, T], F32R)
        kt_lo = ph.sb("kt_lo", [P, KV, T], F32R)
        v_hi = ph.sb("v_hi", [P, QB, HW], F32R)
        v_lo = ph.sb("v_lo", [P, QB, HW], F32R)
        masked = ph.sb("masked", [P, GROUP, SPANS], F32)
        top = ph.sb("top", [P, GROUP, QB], F32)
        minus_top = ph.sb("minus_top", [P, GROUP, QB], F32)
        prob = ph.sb("prob", [P, GROUP, BLOCKS * P], F32)
        total = ph.sb("total", [P, GROUP, QB], F32)
        inverse = ph.sb("inverse", [P, GROUP, QB], F32)
        pt_hi = ph.sb("pt_hi", [P, GROUP, QS], F32R)
        pt_lo = ph.sb("pt_lo", [P, GROUP, QS], F32R)
        ctx_hi = ph.sb("ctx_hi", [P, QB, HW], F32R)
        ctx_lo = ph.sb("ctx_lo", [P, QB, HW], F32R)

        ring = [ph.ps(f"ring{k}") for k in range(RING)]
        out = ph.ps("out")

        set_up = ph.sem("set_up")
        y_turned = ph.sem("y_turned")
        yt_hi_ready = ph.sem("yt_hi_ready")
        yt_ready = ph.sem("yt_ready")
        k_projected = ph.sem("k_projected")
        k_cos_done = ph.sem("k_cos_done")
        k_sin_done = ph.sem("k_sin_done")
        k_squared = ph.sem("k_squared")
        k_added = ph.sem("k_added")
        k_ms_ready = ph.sem("k_ms_ready")
        k_rs_ready = ph.sem("k_rs_ready")
        k_normed = ph.sem("k_normed")
        k_turned = ph.sem("k_turned")
        kt_hi_ready = ph.sem("kt_hi_ready")
        kt_ready = ph.sem("kt_ready")
        v_projected = ph.sem("v_projected")
        v_hi_ready = ph.sem("v_hi_ready")
        v_ready = ph.sem("v_ready")
        q_projected = ph.sem("q_projected")
        q_cos_done = ph.sem("q_cos_done")
        q_sin_done = ph.sem("q_sin_done")
        q_squared = ph.sem("q_squared")
        q_added = ph.sem("q_added")
        q_ms_ready = ph.sem("q_ms_ready")
        q_rs_ready = ph.sem("q_rs_ready")
        q_turned = ph.sem("q_turned")
        qt_hi_ready = ph.sem("qt_hi_ready")
        qt_ready = ph.sem("qt_ready")
        scored = ph.sem("scored")
        top_ready = ph.sem("top_ready")
        bias_ready = ph.sem("bias_ready")
        exp_done = ph.sem("exp_done")
        inverse_ready = ph.sem("inverse_ready")
        prob_ready = ph.sem("prob_ready")
        p_turned = ph.sem("p_turned")
        pt_hi_ready = ph.sem("pt_hi_ready")
        pt_ready = ph.sem("pt_ready")
        ctx_summed = ph.sem("ctx_summed")
        ctx_hi_ready = ph.sem("ctx_hi_ready")
        ctx_ready = ph.sem("ctx_ready")
        projected = ph.sem("projected")
        out_used = ph.sem("out_used")

        def batches(eng, slot):
            def batch(b):
                for g in range(KV):
                    slot(b, g)

            batch(0)
            with eng.Fori(1, BATCH - 1) as b:
                batch(b)
            batch(BATCH - 1)
            slot(BATCH, 0)
            slot(BATCH, 1)

        def by_head(ap):
            return ap.rearrange("p (h d) -> p h d", h=GROUP)

        def add_k(eng, b, t):
            eng.wait_ge(k_sin_done, QB * b + t + 1)
            eng.tensor_tensor(k_cos[:, t, :], k_cos[:, t, :], k_sin[:, t, :], ALU.add).then_inc(k_added, 1)

        def add_q(eng, n, t):
            eng.wait_ge(q_sin_done, QB * n + t + 1)
            eng.tensor_tensor(q_cos[:, t, :], q_cos[:, t, :], q_sin[:, t, :], ALU.add).then_inc(q_added, 1)

        def halves(ap):
            return ap.rearrange("p (h s d) -> p h s d", h=GROUP, s=2)

        with nc.Block() as block:

            @block.tensor
            def _(pe):
                readers = {
                    "S": lambda b, g, h: (top_ready, QB * (GROUP * (KV * b + g) + h + 1)),
                    "J": lambda b, g, t: (q_squared, GROUP * (QB * (KV * b + g + 1) + t + 1)),
                    "K": lambda b, g, t: (k_squared, GROUP * (QB * (b + 1) + t + 1)),
                    "V": lambda b, g, t: (v_ready, QB * b + t + 1),
                    "C": lambda b, g, t: (ctx_ready, QB * (KV * b + g - 2) + t + 1),
                    "P": lambda b, g, h: (pt_ready, GROUP * (KV * b + g - 1) + h + 1),
                    "Y": lambda b, g, _: (yt_ready, b + 2),
                    "T": lambda b, g, t: (kt_ready, QB * (b + 1) + t + 1),
                    "Q": lambda b, g, t: (qt_ready, QB * (KV * b + g + 1) + t + 1),
                }

                def begin(f, what, g, part):
                    before = f.contents_before(what, g, part)
                    if before:
                        (what0, g0, part0), b0 = before
                        pe.wait_ge(*readers[what0](b0, g0, part0))
                    return ring[f.bank(what, g, part)]

                def turn_y(f):
                    b = f.b + 1
                    bank = begin(f, "Y", KV - 2, 0)
                    pe.wait_ge(norm.y_ready, QB * (b + 1))
                    for k in range(KC):
                        for t in range(QB):
                            last = pe.transpose(bank[:, k * T + t * P:k * T + (t + 1) * P], keep.y[:, t, k * P:(k + 1) * P], keep.ident[:, :])
                    last.then_inc(y_turned, 1)

                def project(f, what, g, b, at, done, subs=range(QB)):
                    for t in subs:
                        bank = begin(f, what, g, t)
                        pe.wait_ge(yt_ready, b + 1)
                        parts = []
                        for k in range(KC):
                            tok = slice(t * P, (t + 1) * P)
                            parts += three(yt_hi[:, k, tok], yt_lo[:, k, tok], keep.wqkv_hi[:, k, at:at + HW], keep.wqkv_lo[:, k, at:at + HW])
                        product(pe, bank[:, :], parts).then_inc(done, 1)

                def turn_heads(bank, src, done):
                    for h in range(GROUP):
                        at = slice(h * P, (h + 1) * P)
                        last = pe.transpose(bank[:, at], src[:, at], keep.ident[:, :])
                    last.then_inc(done, 1)

                def turn_q(f, g, subs=range(QB)):
                    for t in subs:
                        bank = begin(f, "Q", g, t)
                        pe.wait_ge(q_added, QB * (KV * f.b + g + 1) + t + 1)
                        turn_heads(bank, q_cos[:, t, :], q_turned)

                def turn_k(f):
                    for t in range(QB):
                        bank = begin(f, "T", KV - 1, t)
                        pe.wait_ge(k_normed, QB * (f.b + 1) + t + 1)
                        turn_heads(bank, k_cos[:, t, :], k_turned)

                def scores(f, g, h):
                    bank = begin(f, "S", g, h)
                    if h == 0:
                        pe.wait_ge(qt_ready, QB * (KV * f.b + g + 1))
                        pe.wait_ge(kt_ready, QB * (f.b + 1))
                    at = slice(h * P, (h + 1) * P)
                    first = 0
                    for t in range(QB):
                        keys = slice((t + 1) * P - SPAN[t], (t + 1) * P)
                        last = product(pe, bank[:, first:first + SPAN[t]],
                                       three(qt_hi[:, t, at], qt_lo[:, t, at], kt_hi[:, g, keys], kt_lo[:, g, keys]))
                        first += SPAN[t]
                    last.then_inc(scored, 1)

                def turn_probs(f, g, h):
                    bank = begin(f, "P", g, h)
                    pe.wait_ge(prob_ready, QB * (GROUP * (KV * f.b + g - 1) + h + 1))
                    for k in range(BLOCKS):
                        q = QUERIES[k]
                        last = pe.transpose(bank[:, Q_AT[k]:Q_AT[k] + q], prob[0:q, h, k * P:(k + 1) * P], keep.ident[0:q, 0:q])
                    last.then_inc(p_turned, 1)

                def context(f, g):
                    n = KV * f.b + g - 2
                    v_at = slice((g - 2) % KV * DH, ((g - 2) % KV + 1) * DH)
                    pe.wait_ge(pt_ready, GROUP * (n + 1))
                    pe.wait_ge(v_ready, QB * (f.b + 1) if g >= 2 else QB * f.b)
                    for t in range(QB):
                        bank = begin(f, "C", g, t)
                        for k in range(t, -1, -1):
                            at = slice(Q_AT[t + k], Q_AT[t + k] + QUERIES[t + k])
                            last = product(pe, by_head(bank[:, :])[:, :, 0:QUERIES[t + k]],
                                           three(v_hi[:, k, v_at], v_lo[:, k, v_at], pt_hi[:, :, at], pt_lo[:, :, at]),
                                           start=(k == t), stop=(k == 0))
                        last.then_inc(ctx_summed, 1)

                def out_projection(b, g, t):
                    n = KV * b + g - 2
                    g = (g - 2) % KV
                    pe.wait_ge(ctx_ready, QB * n + t + 1)
                    if g == 0 and t == 0:
                        wait(pe, out_used, b)
                    for h in range(GROUP):
                        at = slice(h * P, (h + 1) * P)
                        w = slice((g * GROUP + h) * D, (g * GROUP + h + 1) * D)
                        last = product(pe, out[:, t * D:(t + 1) * D],
                                       three(ctx_hi[:, t, at], ctx_lo[:, t, at], keep.wo_hi[:, w], keep.wo_lo[:, w]),
                                       start=(g == 0 and t == 0 and h == 0), stop=(g == KV - 1 and h == GROUP - 1))
                    last.then_inc(projected, 1)

                def slot(b, g):
                    f = Fills(b)
                    here, ahead, turns, sums = stages(b, g)
                    next_q = (b, (g + 1) * HW) if g < KV - 1 else (b + 1, 0)
                    if ahead:
                        project(f, "J", g, *next_q, q_projected, [0])
                    if sums:
                        context(f, g)
                    if turns:
                        turn_probs(f, g, 0)
                        turn_probs(f, g, 1)
                    if ahead:
                        project(f, "J", g, *next_q, q_projected, [1])
                    if turns:
                        turn_probs(f, g, 2)
                        turn_probs(f, g, 3)
                    if ("Y", g, 0) in f.own:
                        turn_y(f)
                    if here:
                        scores(f, g, 0)
                        scores(f, g, 1)
                    if sums:
                        out_projection(b, g, 0)
                    if here:
                        scores(f, g, 2)
                        scores(f, g, 3)
                    if ("V", g, 0) in f.own:
                        project(f, "V", g, b, V_AT, v_projected)
                    if ("K", g, 0) in f.own:
                        project(f, "K", g, b + 1, K_AT, k_projected)
                    if ahead:
                        turn_q(f, g, [0])
                    if sums:
                        out_projection(b, g, 1)
                    if ahead:
                        turn_q(f, g, [1])
                    if ("T", g, 0) in f.own:
                        turn_k(f)

                f = Fills(-1)
                pe.wait_ge(set_up, 1)
                turn_y(f)
                project(f, "K", KV - 2, 0, K_AT, k_projected)
                project(f, "J", KV - 1, 0, 0, q_projected)
                turn_k(f)
                turn_q(f, KV - 1)
                batches(pe, slot)

            @block.scalar
            def _(act):
                def normalise(b):
                    wait(act, y_turned, b)
                    norm.normalise(act, b, range(QB))

                def squares_of(bank, ss, done):
                    for h in range(GROUP):
                        at = slice(h * P, (h + 1) * P)
                        act.activation(bank[:, at], bank[:, at], ACT.Square, accum_out=ss[:, h:h + 1]).then_inc(done, 1)

                def square_k(f):
                    b = f.b + 1
                    wait(act, k_rs_ready, b)
                    for t in range(QB):
                        act.wait_ge(k_sin_done, QB * b + t + 1)
                        squares_of(ring[f.bank("K", KV - 2, t)], k_ss[:, t, :], k_squared)

                def square_q(f, g, subs=range(QB)):
                    n = KV * f.b + g + 1
                    if 0 in subs:
                        wait(act, q_rs_ready, n)
                    for t in subs:
                        act.wait_ge(q_sin_done, QB * n + t + 1)
                        squares_of(ring[f.bank("J", g, t)], q_ss[:, t, :], q_squared)

                def exponentials(b, g, h):
                    n = GROUP * (KV * b + g) + h
                    act.wait_ge(bias_ready, n + 1)
                    wait(act, p_turned, n - GROUP + 1)
                    wait(act, inverse_ready, n - GROUP + 1)
                    first = 0
                    for t in range(QB):
                        to = BLOCKS * P if t else P
                        act.activation(prob[:, h, to - SPAN[t]:to], masked[:, h, first:first + SPAN[t]], ACT.Exp,
                                       bias=minus_top[:, h, t:t + 1], scale=q_rs[:, g % 2, t, h:h + 1],
                                       accum_out=total[:, h, t:t + 1]).then_inc(exp_done, 1)
                        first += SPAN[t]

                def high_y(f):
                    b = f.b + 1
                    act.wait_ge(y_turned, b + 1)
                    wait(act, q_projected, QB * KV * b)
                    act.activation(yt_hi[:, :, :], ring[f.bank("Y", KV - 2, 0)][:, :].rearrange("p (k t) -> p k t", k=KC), ACT.Copy).then_inc(yt_hi_ready, 1)

                def high_k(f):
                    b = f.b + 1
                    wait(act, scored, GROUP * KV * b)
                    for t in range(QB):
                        act.wait_ge(k_turned, QB * b + t + 1)
                        act.activation(kt_hi[:, :, t * P:(t + 1) * P], by_head(ring[f.bank("T", KV - 1, t)][:, :]), ACT.Copy).then_inc(kt_hi_ready, 1)

                def high_v(f):
                    wait(act, ctx_summed, QB * KV * f.b)
                    for t in range(QB):
                        act.wait_ge(v_projected, QB * f.b + t + 1)
                        act.activation(v_hi[:, t, :], ring[f.bank("V", 1, t)][:, :], ACT.Copy).then_inc(v_hi_ready, 1)

                def high_q(f, g, subs=range(QB)):
                    n = KV * f.b + g + 1
                    wait(act, scored, GROUP * n)
                    for t in subs:
                        act.wait_ge(q_turned, QB * n + t + 1)
                        act.activation(qt_hi[:, t, :], ring[f.bank("Q", g, t)][:, :], ACT.Copy).then_inc(qt_hi_ready, 1)

                def high_p(f, g, h):
                    n = KV * f.b + g - 1
                    act.wait_ge(p_turned, GROUP * n + h + 1)
                    wait(act, ctx_summed, QB * n)
                    act.activation(pt_hi[:, h, :], ring[f.bank("P", g, h)][:, 0:QS], ACT.Copy).then_inc(pt_hi_ready, 1)

                def high_c(f, g):
                    n = KV * f.b + g - 2
                    for t in range(QB):
                        act.wait_ge(ctx_summed, QB * n + t + 1)
                        wait(act, projected, QB * (n - 1) + t + 1)
                        act.activation(ctx_hi[:, t, :], ring[f.bank("C", g, t)][:, :], ACT.Copy).then_inc(ctx_hi_ready, 1)

                def slot(b, g):
                    f = Fills(b)
                    here, ahead, turns, sums = stages(b, g)
                    if sums:
                        high_c(f, g)
                    if ahead:
                        square_q(f, g, [0])
                    if turns:
                        high_p(f, g, 0)
                        high_p(f, g, 1)
                        high_p(f, g, 2)
                        high_p(f, g, 3)
                    if ("Y", g, 0) in f.own:
                        high_y(f)
                    if ahead:
                        square_q(f, g, [1])
                    if here:
                        exponentials(b, g, 0)
                        exponentials(b, g, 1)
                        exponentials(b, g, 2)
                        exponentials(b, g, 3)
                    if ("V", g, 0) in f.own:
                        high_v(f)
                        if stages(b + 1, 0)[0]:
                            normalise(b + 1)
                        else:
                            act.wait_ge(y_turned, BATCH)
                            next_norm.normalise(act, 0, range(next_norm.subs))
                    if ("K", g, 0) in f.own:
                        square_k(f)
                    if ahead:
                        high_q(f, g)
                    if ("T", g, 0) in f.own:
                        high_k(f)

                f = Fills(-1)
                high_y(f)
                square_k(f)
                square_q(f, KV - 1)
                high_k(f)
                high_q(f, KV - 1)
                batches(act, slot)

            @block.vector
            def _(dve):
                def rope(bank, table, t, by_cos, by_sin, cos_done, sin_done):
                    cos = keep.rope[:, table, 0, t, :]
                    sin = keep.rope[:, table, 1, t, :].rearrange("p (s d) -> p s d", s=2)
                    dve.tensor_tensor(by_head(by_cos[:, t, :]), by_head(bank[:, :]), cos[:, None, :].broadcast_to([P, GROUP, P]), ALU.mult).then_inc(cos_done, 1)
                    dve.tensor_tensor(halves(by_sin[:, t, :]), halves(bank[:, :])[:, :, ::-1, :],
                                      sin[:, None, :, :].broadcast_to([P, GROUP, 2, P // 2]), ALU.mult).then_inc(sin_done, 1)

                def rope_k(f):
                    b = f.b + 1
                    for t in range(QB):
                        dve.wait_ge(k_projected, QB * b + t + 1)
                        wait(dve, k_turned, QB * (b - 1) + t + 1)
                        rope(ring[f.bank("K", KV - 2, t)], 1, t, k_cos, k_sin, k_cos_done, k_sin_done)

                def rope_q(f, g, t):
                    n = KV * f.b + g + 1
                    dve.wait_ge(q_projected, QB * n + t + 1)
                    wait(dve, q_turned, QB * (n - 1) + t + 1)
                    rope(ring[f.bank("J", g, t)], 0, t, q_cos, q_sin, q_cos_done, q_sin_done)

                def maxima(f, g, h):
                    n = GROUP * (KV * f.b + g) + h
                    bank = ring[f.bank("S", g, h)]
                    dve.wait_ge(scored, n + 1)
                    wait(dve, exp_done, QB * (n - GROUP + 1))
                    stand(dve)
                    first = 0
                    for t in range(QB):
                        at = slice(first, first + SPAN[t])
                        dve.tensor_tensor_reduce(masked[:, h, at], bank[:, at], keep.mask[:, at], 1.0, -3e38, ALU.add, ALU.max,
                                                 top[:, h, t:t + 1]).then_inc(top_ready, 1)
                        first += SPAN[t]
                    dve.wait_ge(top_ready, QB * (n + 1))
                    if h == 0:
                        dve.wait_ge(q_rs_ready, KV * f.b + g + 1)
                    dve.scalar_tensor_tensor(minus_top[:, h, :], top[:, h, :], -1.0, q_rs[:, g % 2, :, h], ALU.mult, ALU.mult).then_inc(bias_ready, 1)

                def invert_totals(n, heads):
                    for h in heads:
                        dve.wait_ge(exp_done, QB * (GROUP * n + h + 1))
                        wait(dve, prob_ready, QB * (GROUP * (n - 1) + h + 1))
                        dve.reciprocal(inverse[:, h, :], total[:, h, :]).then_inc(inverse_ready, 1)

                def low(dst, hi, src, done):
                    dve.tensor_tensor(dst, src, hi.bitcast(F32), ALU.subtract).then_inc(done, 1)

                def low_y(f):
                    dve.wait_ge(yt_hi_ready, f.b + 2)
                    low(yt_lo[:, :, :], yt_hi[:, :, :], ring[f.bank("Y", KV - 2, 0)][:, :].rearrange("p (k t) -> p k t", k=KC), yt_ready)

                def low_k(f):
                    for t in range(QB):
                        at = slice(t * P, (t + 1) * P)
                        dve.wait_ge(kt_hi_ready, QB * (f.b + 1) + t + 1)
                        low(kt_lo[:, :, at], kt_hi[:, :, at], by_head(ring[f.bank("T", KV - 1, t)][:, :]), kt_ready)

                def low_v(f):
                    for t in range(QB):
                        dve.wait_ge(v_hi_ready, QB * f.b + t + 1)
                        low(v_lo[:, t, :], v_hi[:, t, :], ring[f.bank("V", 1, t)][:, :], v_ready)

                def low_q(f, g, subs=range(QB)):
                    n = KV * f.b + g + 1
                    for t in subs:
                        dve.wait_ge(qt_hi_ready, QB * n + t + 1)
                        low(qt_lo[:, t, :], qt_hi[:, t, :], ring[f.bank("Q", g, t)][:, :], qt_ready)

                def low_p(f, g, h):
                    dve.wait_ge(pt_hi_ready, GROUP * (KV * f.b + g - 1) + h + 1)
                    low(pt_lo[:, h, :], pt_hi[:, h, :], ring[f.bank("P", g, h)][:, 0:QS], pt_ready)

                def low_c(f, g):
                    n = KV * f.b + g - 2
                    for t in range(QB):
                        dve.wait_ge(ctx_hi_ready, QB * n + t + 1)
                        low(ctx_lo[:, t, :], ctx_hi[:, t, :], ring[f.bank("C", g, t)][:, :], ctx_ready)

                def add_output(b):
                    dve.wait_ge(projected, QB * KV * (b + 1))
                    at = keep.x[:, bass.ds(b * QB, QB), :].rearrange("p t d -> p (t d)")
                    dve.tensor_tensor(at, out[:, :], at, ALU.add).then_inc(out_used, 1)

                def slot(b, g):
                    f = Fills(b)
                    here, ahead, turns, sums = stages(b, g)
                    if here and g == 0:
                        low_q(Fills(b - 1), KV - 1)
                    if ahead:
                        rope_q(f, g, 0)
                    if here and g == 0:
                        low_k(Fills(b - 1))
                    elif here:
                        low_q(f, g - 1)
                    if sums:
                        low_c(f, g)
                    if g == 2 and sums and not (isinstance(b, int) and b == 0):
                        add_output(b - 1)
                    if turns:
                        low_p(f, g, 0)
                        low_p(f, g, 1)
                    if ahead:
                        rope_q(f, g, 1)
                    if turns:
                        low_p(f, g, 2)
                    if ("Y", g, 0) in f.own:
                        low_y(f)
                    if here:
                        maxima(f, g, 0)
                    if turns:
                        low_p(f, g, 3)
                    if here:
                        maxima(f, g, 1)
                        maxima(f, g, 2)
                        maxima(f, g, 3)
                        invert_totals(KV * b + g, (0, 1))
                    if g == 0 and stages(b + 1, 0)[0]:
                        norm.statistics(dve, b + 1)
                    elif g == 0 and here:
                        dve.wait_ge(norm.nmr_ready, BATCH)
                        dve.wait_ge(out_used, next_norm.subs // QB)
                        next_norm.statistics(dve, 0)
                    elif g == 2 and here and not stages(b + 1, 0)[0]:
                        dve.wait_ge(out_used, 2 * next_norm.subs // QB)
                        next_norm.statistics(dve, 1)
                    if ("V", g, 0) in f.own:
                        low_v(f)
                    if ("K", g, 0) in f.own:
                        rope_k(f)
                    if here:
                        invert_totals(KV * b + g, (2, 3))

                f = Fills(-1)
                low_y(f)
                rope_k(f)
                add_k(dve, 0, 0)
                add_k(dve, 0, 1)
                rope_q(f, KV - 1, 0)
                rope_q(f, KV - 1, 1)
                add_q(dve, 0, 0)
                add_q(dve, 0, 1)
                batches(dve, slot)
                add_output(BATCH - 1)
                dve.wait_ge(out_used, BATCH)

            @block.gpsimd
            def _(pool):
                def rs_of_k(b):
                    pool.wait_ge(k_squared, GROUP * QB * (b + 1))
                    stand(pool)
                    pool.tensor_scalar(k_ms[:, :, :], k_ss[:, :, :], 1.0 / DH, RMS_EPS, ALU.mult, ALU.add).then_inc(k_ms_ready, 1)
                    pool.wait_ge(k_ms_ready, b + 1)
                    pool.tensor_tensor(k_rs[:, :, :], k_ms[:, :, :], keep.power[:, :, :], ALU.pow).then_inc(k_rs_ready, 1)

                def scale_k(b, t):
                    pool.wait_ge(k_rs_ready, b + 1)
                    pool.wait_ge(k_added, QB * b + t + 1)
                    pool.tensor_tensor(by_head(k_cos[:, t, :]), by_head(k_cos[:, t, :]), k_rs[:, t, :, None].broadcast_to([P, KV, DH]), ALU.mult).then_inc(k_normed, 1)

                def norm_q(n, parity):
                    pool.wait_ge(q_squared, GROUP * QB * (n + 1))
                    stand(pool)
                    pool.tensor_scalar(q_ms[:, :, :], q_ss[:, :, :], 1.0, DH * RMS_EPS, ALU.mult, ALU.add).then_inc(q_ms_ready, 1)
                    pool.wait_ge(q_ms_ready, n + 1)
                    wait(pool, exp_done, QB * GROUP * (n - 1))
                    pool.tensor_tensor(q_rs[:, parity, :, :], q_ms[:, :, :], keep.power[:, :, :], ALU.pow).then_inc(q_rs_ready, 1)

                def scale_probs(n, heads):
                    for h in heads:
                        pool.wait_ge(inverse_ready, GROUP * n + h + 1)
                        stand(pool)
                        for t in range(QB):
                            to = BLOCKS * P if t else P
                            at = prob[:, h, to - SPAN[t]:to]
                            pool.tensor_scalar(at, at, inverse[:, h, t:t + 1], 1.0, ALU.mult, ALU.mult).then_inc(prob_ready, 1)

                def slot(b, g):
                    f = Fills(b)
                    here, ahead, turns, sums = stages(b, g)
                    n = KV * b + g
                    if ahead:
                        add_q(pool, n + 1, 0)
                    if ("T", g, 0) in f.own:
                        rs_of_k(b + 1)
                        scale_k(b + 1, 0)
                    if ahead:
                        add_q(pool, n + 1, 1)
                    if ("T", g, 0) in f.own:
                        scale_k(b + 1, 1)
                    if ahead:
                        norm_q(n + 1, (g + 1) % 2)
                    if ("V", g, 0) in f.own and stages(b + 1, 0)[0]:
                        norm.rstd_of(pool, b + 1)
                    elif ("V", g, 0) in f.own:
                        pool.wait_ge(norm.y_ready, QB * BATCH)
                        next_norm.rstd_of(pool, 0)
                    elif g == KV - 1 and here and not ahead:
                        next_norm.rstd_of(pool, 1)
                    if here:
                        scale_probs(n, (0, 1))
                    if ("K", g, 0) in f.own:
                        add_k(pool, b + 1, 0)
                        add_k(pool, b + 1, 1)
                    if here:
                        scale_probs(n, (2, 3))

                pool.memset(prob[:, :, P:2 * P], 0.0).then_inc(set_up, 1)
                pool.wait_ge(set_up, 1)
                rs_of_k(0)
                scale_k(0, 0)
                scale_k(0, 1)
                norm_q(0, 0)
                batches(pool, slot)


class Kept:

    def __init__(self, nc, stack):
        def sb(name, shape, dt):
            return stack.enter_context(nc.sbuf_tensor(name, shape, dt))

        self.x = sb("x", [P, SUB, D], F32)
        with ExitStack() as early:
            self.early = [early.enter_context(nc.sbuf_tensor(name, shape, F32)) for name, shape in (
                ("raw8", [P, M, 3 * D]), ("magic", [P, 2, 3 * D]), ("q8", [P, 2, 3 * D]), ("over", [P, 2, 3 * D]),
                ("raw_scale", [P, 2, M]), ("down_s", [P, D]), ("wrow", [P, 2, DH]), ("rope_raw", [P, 2, 2, DH]))]
        self.wqkv_hi = sb("wqkv_hi", [P, KC, QKV], F32R)
        self.wqkv_lo = sb("wqkv_lo", [P, KC, QKV], F32R)
        self.wo_hi = sb("wo_hi", [P, HEADS * D], F32R)
        self.wo_lo = sb("wo_lo", [P, HEADS * D], F32R)
        self.y = sb("y", [P, FFN_SUBS, D], F32)
        self.stats = sb("stats", [P, FFN_SUBS, 6], F32)
        self.mv = sb("mv", [P, FFN_SUBS, 2], F32)
        self.var = sb("var", [P, FFN_SUBS], F32)
        self.rstd = sb("rstd", [P, FFN_SUBS], F32)
        self.nmr = sb("nmr", [P, FFN_SUBS], F32)
        self.power = sb("power", [P, T // P, GROUP], F32)
        self.w8 = sb("w8", [P, M, 3 * D], BF16)
        self.gate_half = sb("gate_half", [P, M], F32)
        self.gate_up = sb("gate_up", [P, M], F32)
        self.down_half = sb("down_half", [P, D], F32)
        self.rope = sb("rope", [P, 2, 2, 2, DH], F32)
        self.ident = sb("ident", [P, P], F32)
        self.mask = sb("mask", [P, 2 * P + WINDOW], F32)


def build(nc, dram, out):
    with ExitStack() as stack:
        keep = Kept(nc, stack)
        first, middle, second = (Norm(nc, stack, keep, prefix, subs) for prefix, subs in (("f_", FFN_SUBS), ("a_", T // P), ("g_", FFN_SUBS)))
        ffn_phase(nc, stack, keep, "f_", first, middle, dram=dram)
        attention_phase(nc, stack, keep, middle, second)
        ffn_phase(nc, stack, keep, "g_", second, out_dram=out)


def constants():
    inv_freq = (1.0 / np.float32(10000.0) ** (np.arange(0, DH, 2, dtype=np.float32) / np.float32(DH))).astype(np.float32)
    freqs = np.arange(T, dtype=np.float32)[:, None] * inv_freq[None, :]
    cos, sin = np.cos(freqs), np.sin(freqs)
    q, k0, k1 = np.arange(P)[:, None], np.arange(P)[None, :], np.arange(-WINDOW, P)[None, :]
    seen = np.concatenate([(q >= k0) & (q - k0 <= WINDOW), (q >= k1) & (q - k1 <= WINDOW)], axis=1)
    return {
        "cos": np.concatenate([cos, cos], axis=1),
        "sin": np.concatenate([-sin, sin], axis=1),
        "mask": np.where(seen, np.float32(0), np.float32(MASKED)),
        "ident": np.eye(P, dtype=np.float32),
    }


def kernel(L0_attn_x, L0_attn_Wq, L0_attn_Wk, L0_attn_Wv, L0_attn_Wo, L0_attn_qn_w, L0_attn_kn_w,
           L0_ffn_gate_w, L0_ffn_up_w, L0_ffn_down_w, L0_ffn_gate_scale, L0_ffn_up_scale, L0_ffn_down_scale):
    import concourse.bacc as bacc
    from concourse.bass_utils import run_bass_kernel_spmd

    given = {
        "x": L0_attn_x,
        "wqkv_t": np.concatenate([L0_attn_Wq, L0_attn_Wk, L0_attn_Wv], axis=0).T,
        "wo_t": np.asarray(L0_attn_Wo).T,
        "qn": L0_attn_qn_w, "kn": L0_attn_kn_w,
        "gate_w": L0_ffn_gate_w, "up_w": L0_ffn_up_w, "down_w": L0_ffn_down_w,
        "gate_s": np.asarray(L0_ffn_gate_scale).reshape(M, P).T, "up_s": np.asarray(L0_ffn_up_scale).reshape(M, P).T, "down_s": L0_ffn_down_scale,
    }
    given.update(constants())
    nc = bacc.Bacc("TRN2", target_bir_lowering=False, num_devices=1)
    arrays, dram = {}, {}
    for name, a in given.items():
        a = np.ascontiguousarray(a)
        arrays[f"in_{name}"] = a
        dram[name] = nc.dram_tensor(f"in_{name}", a.shape, mybir.dt.from_np(a.dtype), kind="ExternalInput").ap()
    out = nc.dram_tensor("out", (BATCH, T, D), F32, kind="ExternalOutput").ap()
    build(nc, dram, out)
    return run_bass_kernel_spmd(nc, [arrays], core_ids=[0]).results[0]["out"]
```
